# Optimizing a Trainium2 kernel written in Bass

```python
import numpy as np
import jax
import jax.numpy as jnp

def _softmax(x, axis=-1):
    return jax.nn.softmax(x, axis=axis)

def _gelu(x):
    return jax.nn.gelu(x, approximate=True)

def _silu(x):
    return jax.nn.silu(x)

def _sigmoid(x):
    return jax.nn.sigmoid(x)

def _layernorm(x, axis=-1, eps=1e-05):
    m = jnp.mean(x, axis=axis, keepdims=True)
    v = jnp.var(x, axis=axis, keepdims=True)
    return (x - m) / jnp.sqrt(v + eps)

def _scatter_add(tgt, idx, src, axis=0):
    return tgt.at[idx].add(src)

def _segment_sum(src, seg, n):
    return jax.ops.segment_sum(src, seg, n)
kernel_name = 'mk_perceiver_d1_seqx_r8_a9fd08'

def setup_inputs(seed: int=0):
    np.random.seed(seed)
    _w = jnp.asarray

    def _rec_inputs():
        import jax
        import jax.numpy as jnp
        _rk = jax.random.key(seed)
        x = -0.0002928 + 1 * jax.random.normal(jax.random.fold_in(_rk, 1), (16, 64, 128), jnp.float32)
        _lenS = 64 - jax.random.randint(jax.random.fold_in(_rk, 7), (16,), 0, max(1, 64 // 4) + 1, jnp.int32)
        _lenS2 = 1601 - jax.random.randint(jax.random.fold_in(_rk, 8), (16,), 0, max(1, 1601 // 4) + 1, jnp.int32)
        _ctx_1024P = jax.random.normal(jax.random.fold_in(_rk, 11), (16, 16, 128), jnp.float32)
        _ctx_1024c = jax.random.dirichlet(jax.random.fold_in(_rk, 511), 0.3 * jnp.ones((16,), jnp.float32), (16, 1601))
        _ctx_1024t = jnp.einsum('bsk,bkd->bsd', _ctx_1024c, _ctx_1024P)
        _ctx_1024t = _ctx_1024t * jax.lax.rsqrt(jnp.mean(jnp.square(_ctx_1024t)) + 1e-12) * 0.953939
        ctx_1024 = -1.39393e-06 + 0.999914 * (_ctx_1024t + 0.3 * jax.random.normal(jax.random.fold_in(_rk, 611), (16, 1601, 128), jnp.float32))
        _validS = jnp.arange(64)[None, :] < _lenS[:, None]
        _validS2 = jnp.arange(1601)[None, :] < _lenS2[:, None]
        _causal = jnp.tril(jnp.ones((64, 64), dtype=bool))
        mask_BxSxS2_if1 = jnp.where(jnp.ones((16, 64, 1601), dtype=bool), 1, 0).astype(jnp.int32)
        return (x, ctx_1024, mask_BxSxS2_if1)
    x, ctx_1024, mask_BxSxS2_if1 = _rec_inputs()

    def _L0_xattn_setup():
        import jax, jax.numpy as jnp
        import numpy as np
        N_HEAD = 16
        N_FEAT = 128
        D_K = N_FEAT // N_HEAD
        key = jax.random.key(seed)
        ks = jax.random.split(key, 11)
        B, T1, T2 = (2, 256, 256)
        s = 0.02
        return {'query': jax.random.normal(ks[0], (B, T1, N_FEAT), jnp.float32), 'key_': jax.random.normal(ks[1], (B, T2, N_FEAT), jnp.float32), 'value': jax.random.normal(ks[2], (B, T2, N_FEAT), jnp.float32), 'mask': jnp.ones((B, T1, T2), jnp.int32), 'Wq': jax.random.normal(ks[3], (N_FEAT, N_FEAT), jnp.float32) * s, 'bq': jnp.zeros((N_FEAT,), jnp.float32), 'Wk': jax.random.normal(ks[4], (N_FEAT, N_FEAT), jnp.float32) * s, 'bk': jnp.zeros((N_FEAT,), jnp.float32), 'Wv': jax.random.normal(ks[5], (N_FEAT, N_FEAT), jnp.float32) * s, 'bv': jnp.zeros((N_FEAT,), jnp.float32), 'Wo': jax.random.normal(ks[6], (N_FEAT, N_FEAT), jnp.float32) * s, 'bo': jnp.zeros((N_FEAT,), jnp.float32)}
    _L0_xattn_all = _L0_xattn_setup()
    _L0_xattn_in = {k: v for k, v in _L0_xattn_all.items() if k in ('Wq', 'bq', 'Wk', 'bk', 'Wv', 'bv', 'Wo', 'bo')}
    del _L0_xattn_all

    def _L0_attn_setup():
        import jax, jax.numpy as jnp
        import numpy as np
        N_HEADS = 16
        KV_HEADS = 4
        D_HEAD = 64
        D_MODEL = 128
        NUM_BUCKETS = 32
        MAX_DISTANCE = 128

        def _relative_position_bucket(relative_position, num_buckets=NUM_BUCKETS, max_distance=MAX_DISTANCE):
            nb = num_buckets // 2
            rel_buckets = (relative_position > 0).astype(jnp.int32) * nb
            rp = jnp.abs(relative_position)
            max_exact = nb // 2
            is_small = rp < max_exact
            rp_safe = jnp.maximum(rp, 1).astype(jnp.float32)
            rp_large = max_exact + (jnp.log(rp_safe / max_exact) / np.log(max_distance / max_exact) * (nb - max_exact)).astype(jnp.int32)
            rp_large = jnp.minimum(rp_large, nb - 1)
            return rel_buckets + jnp.where(is_small, rp, rp_large)

        def compute_bias(rel_bias, q_len, k_len):
            context_pos = jnp.arange(q_len)[:, None]
            memory_pos = jnp.arange(k_len)[None, :]
            buckets = _relative_position_bucket(memory_pos - context_pos)
            values = rel_bias[buckets]
            return jnp.transpose(values, (2, 0, 1))[None]
        key = jax.random.key(seed)
        ks = jax.random.split(key, 6)
        scale = D_MODEL ** (-0.5)
        return {'hidden_states': jax.random.normal(ks[0], (4, 256, D_MODEL), jnp.float32), 'Wq': jax.random.normal(ks[1], (N_HEADS * D_HEAD, D_MODEL), jnp.float32) * scale, 'Wk': jax.random.normal(ks[2], (N_HEADS * D_HEAD, D_MODEL), jnp.float32) * scale, 'Wv': jax.random.normal(ks[3], (N_HEADS * D_HEAD, D_MODEL), jnp.float32) * scale, 'Wo': jax.random.normal(ks[4], (D_MODEL, N_HEADS * D_HEAD), jnp.float32) * scale, 'rel_bias': jax.random.normal(ks[5], (NUM_BUCKETS, N_HEADS), jnp.float32)}
    _L0_attn_all = _L0_attn_setup()
    _L0_attn_in = {k: v for k, v in _L0_attn_all.items() if k in ('Wq', 'Wk', 'Wv', 'Wo', 'rel_bias')}
    del _L0_attn_all

    def _L0_ffn_setup():
        import jax, jax.numpy as jnp
        import numpy as np
        NEG_INF = -1e+30

        def _moe_forward(x, router_w, router_b, w1, b1, w2, b2, top_k=2):
            B, S, D = x.shape
            E = router_w.shape[1]
            logits = jnp.einsum('bsd,de->bse', x, router_w) + router_b
            top_vals, top_idx = jax.lax.top_k(logits, top_k)
            keep = jax.nn.one_hot(top_idx, E, dtype=logits.dtype).sum(-2) > 0
            sparse_logits = jnp.where(keep, logits, NEG_INF)
            gating = jax.nn.softmax(sparse_logits, axis=-1)
            xf = x.reshape(-1, D)
            gf = gating.reshape(-1, E)
            h = jax.nn.relu(jnp.einsum('td,edh->eth', xf, w1) + b1[:, None, :])
            y = jnp.einsum('eth,ehd->etd', h, w2) + b2[:, None, :]
            out = jnp.einsum('etd,te->td', y, gf)
            return out.reshape(B, S, D)
        key = jax.random.key(seed)
        ks = jax.random.split(key, 5)
        B, S, D, E, H = (2, 256, 128, 8, 512)
        scale = 0.02
        return {'x': jax.random.normal(ks[0], (B, S, D), dtype=jnp.float32), 'router_w': jax.random.normal(ks[1], (D, E), dtype=jnp.float32) * scale, 'router_b': jnp.zeros((E,), dtype=jnp.float32), 'w1': jax.random.normal(ks[2], (E, D, H), dtype=jnp.float32) * scale, 'b1': jnp.zeros((E, H), dtype=jnp.float32), 'w2': jax.random.normal(ks[3], (E, H, D), dtype=jnp.float32) * scale, 'b2': jnp.zeros((E, D), dtype=jnp.float32)}
    _L0_ffn_all = _L0_ffn_setup()
    _L0_ffn_in = {k: v for k, v in _L0_ffn_all.items() if k in ('router_w', 'router_b', 'w1', 'b1', 'w2', 'b2')}
    del _L0_ffn_all
    return {'x': x, 'ctx_1024': ctx_1024, 'mask_BxSxS2_if1': mask_BxSxS2_if1, 'L0_xattn_Wq': _L0_xattn_in['Wq'], 'L0_xattn_bq': _L0_xattn_in['bq'], 'L0_xattn_Wk': _L0_xattn_in['Wk'], 'L0_xattn_bk': _L0_xattn_in['bk'], 'L0_xattn_Wv': _L0_xattn_in['Wv'], 'L0_xattn_bv': _L0_xattn_in['bv'], 'L0_xattn_Wo': _L0_xattn_in['Wo'], 'L0_xattn_bo': _L0_xattn_in['bo'], 'L0_attn_Wq': _L0_attn_in['Wq'], 'L0_attn_Wk': _L0_attn_in['Wk'], 'L0_attn_Wv': _L0_attn_in['Wv'], 'L0_attn_Wo': _L0_attn_in['Wo'], 'L0_attn_rel_bias': _L0_attn_in['rel_bias'], 'L0_ffn_router_w': _L0_ffn_in['router_w'], 'L0_ffn_router_b': _L0_ffn_in['router_b'], 'L0_ffn_w1': _L0_ffn_in['w1'], 'L0_ffn_b1': _L0_ffn_in['b1'], 'L0_ffn_w2': _L0_ffn_in['w2'], 'L0_ffn_b2': _L0_ffn_in['b2']}

def reference(x, ctx_1024, mask_BxSxS2_if1, L0_xattn_Wq, L0_xattn_bq, L0_xattn_Wk, L0_xattn_bk, L0_xattn_Wv, L0_xattn_bv, L0_xattn_Wo, L0_xattn_bo, L0_attn_Wq, L0_attn_Wk, L0_attn_Wv, L0_attn_Wo, L0_attn_rel_bias, L0_ffn_router_w, L0_ffn_router_b, L0_ffn_w1, L0_ffn_b1, L0_ffn_w2, L0_ffn_b2):
    import jax
    import jax.numpy as jnp

    def _L0_xattn_ref(query, key_, value, mask, Wq, bq, Wk, bk, Wv, bv, Wo, bo):
        import jax, jax.numpy as jnp
        import numpy as np
        N_HEAD = 16
        N_FEAT = 128
        D_K = N_FEAT // N_HEAD
        B = query.shape[0]

        def heads(x, W, b):
            y = x @ W + b
            return y.reshape(B, -1, N_HEAD, D_K).transpose(0, 2, 1, 3)
        q = heads(query, Wq, bq)
        k = heads(key_, Wk, bk)
        v = heads(value, Wv, bv)
        scale = jnp.sqrt(jnp.asarray(D_K, jnp.float32))
        scores = jnp.einsum('bhqd,bhkd->bhqk', q, k) / scale
        m = mask[:, None, :, :]
        scores = jnp.where(m > 0, scores, jnp.asarray(-10000.0, scores.dtype))
        attn = jax.nn.softmax(scores, axis=-1)
        x = jnp.einsum('bhqk,bhkd->bhqd', attn, v)
        x = x.transpose(0, 2, 1, 3).reshape(B, -1, N_FEAT)
        return x @ Wo + bo

    def _L0_attn_ref(hidden_states, Wq, Wk, Wv, Wo, rel_bias):
        import jax, jax.numpy as jnp
        import numpy as np
        N_HEADS = 16
        KV_HEADS = 4
        D_HEAD = 64
        D_MODEL = 128
        NUM_BUCKETS = 32
        MAX_DISTANCE = 128

        def _relative_position_bucket(relative_position, num_buckets=NUM_BUCKETS, max_distance=MAX_DISTANCE):
            nb = num_buckets // 2
            rel_buckets = (relative_position > 0).astype(jnp.int32) * nb
            rp = jnp.abs(relative_position)
            max_exact = nb // 2
            is_small = rp < max_exact
            rp_safe = jnp.maximum(rp, 1).astype(jnp.float32)
            rp_large = max_exact + (jnp.log(rp_safe / max_exact) / np.log(max_distance / max_exact) * (nb - max_exact)).astype(jnp.int32)
            rp_large = jnp.minimum(rp_large, nb - 1)
            return rel_buckets + jnp.where(is_small, rp, rp_large)

        def compute_bias(rel_bias, q_len, k_len):
            context_pos = jnp.arange(q_len)[:, None]
            memory_pos = jnp.arange(k_len)[None, :]
            buckets = _relative_position_bucket(memory_pos - context_pos)
            values = rel_bias[buckets]
            return jnp.transpose(values, (2, 0, 1))[None]
        B, N, _ = hidden_states.shape
        G = N_HEADS // KV_HEADS
        q = (hidden_states @ Wq.T).reshape(B, N, N_HEADS, D_HEAD).transpose(0, 2, 1, 3)
        k = (hidden_states @ Wk.T).reshape(B, N, N_HEADS, D_HEAD).transpose(0, 2, 1, 3)
        v = (hidden_states @ Wv.T).reshape(B, N, N_HEADS, D_HEAD).transpose(0, 2, 1, 3)
        gq = q.reshape(B, G, KV_HEADS, N, D_HEAD)
        gk = k.reshape(B, G, KV_HEADS, N, D_HEAD).mean(axis=1)
        gv = v.reshape(B, G, KV_HEADS, N, D_HEAD).mean(axis=1)
        scores = jnp.einsum('bghnd,bhsd->bhns', gq, gk)
        bias = compute_bias(rel_bias, N, N)
        gbias = bias.reshape(1, G, KV_HEADS, N, N).mean(axis=1)
        scores = scores + gbias
        attn = jax.nn.softmax(scores.astype(jnp.float32), axis=-1).astype(scores.dtype)
        out = jnp.einsum('bhns,bhsd->bhnd', attn, gv)
        out = out.transpose(0, 2, 1, 3).reshape(B, N, KV_HEADS * D_HEAD)
        out = jnp.tile(out, (1, 1, G))
        return out @ Wo.T

    def _L0_ffn_ref(x, router_w, router_b, w1, b1, w2, b2):
        import jax, jax.numpy as jnp
        import numpy as np
        NEG_INF = -1e+30

        def _moe_forward(x, router_w, router_b, w1, b1, w2, b2, top_k=2):
            B, S, D = x.shape
            E = router_w.shape[1]
            logits = jnp.einsum('bsd,de->bse', x, router_w) + router_b
            top_vals, top_idx = jax.lax.top_k(logits, top_k)
            keep = jax.nn.one_hot(top_idx, E, dtype=logits.dtype).sum(-2) > 0
            sparse_logits = jnp.where(keep, logits, NEG_INF)
            gating = jax.nn.softmax(sparse_logits, axis=-1)
            xf = x.reshape(-1, D)
            gf = gating.reshape(-1, E)
            h = jax.nn.relu(jnp.einsum('td,edh->eth', xf, w1) + b1[:, None, :])
            y = jnp.einsum('eth,ehd->etd', h, w2) + b2[:, None, :]
            out = jnp.einsum('etd,te->td', y, gf)
            return out.reshape(B, S, D)
        return _moe_forward(x, router_w, router_b, w1, b1, w2, b2, top_k=2)
    x = x + _L0_xattn_ref(_layernorm(x, axis=-1), ctx_1024, ctx_1024, mask_BxSxS2_if1, L0_xattn_Wq, L0_xattn_bq, L0_xattn_Wk, L0_xattn_bk, L0_xattn_Wv, L0_xattn_bv, L0_xattn_Wo, L0_xattn_bo)
    x = x + _L0_attn_ref(_layernorm(x, axis=-1), L0_attn_Wq, L0_attn_Wk, L0_attn_Wv, L0_attn_Wo, L0_attn_rel_bias)
    x = x + _L0_ffn_ref(_layernorm(x, axis=-1), L0_ffn_router_w, L0_ffn_router_b, L0_ffn_w1, L0_ffn_b1, L0_ffn_w2, L0_ffn_b2)
    return x

_drawn_inputs = setup_inputs


def setup_inputs(seed=0):
    import zlib

    import numpy as np

    out = dict(_drawn_inputs(seed))
    spreads = {'L0_xattn_bq': (0.0, 0.8),
     'L0_xattn_bk': (0.0, 0.8),
     'L0_xattn_bv': (0.0, 0.1),
     'L0_xattn_bo': (0.0, 0.1),
     'L0_ffn_router_b': (0.0, 0.1),
     'L0_ffn_b1': (0.0, 0.581),
     'L0_ffn_b2': (0.0, 0.1)}
    factors = {'L0_xattn_Wq': 8.0, 'L0_xattn_Wk': 8.0}
    for name, (base, spread) in spreads.items():
        noise = np.random.default_rng([zlib.crc32(name.encode()), seed]).standard_normal(out[name].shape)
        drawn = base * np.exp(spread * noise) if base else spread * noise
        out[name] = jnp.asarray(drawn.astype(out[name].dtype))
    for name, factor in factors.items():
        out[name] = (out[name] * factor).astype(out[name].dtype)
    return out
```

```python
from contextlib import ExitStack

import concourse.bass as bass
from concourse import mybir

F32 = mybir.dt.float32
F32R = mybir.dt.float32r
BF16 = mybir.dt.bfloat16
I32 = mybir.dt.int32
U32 = mybir.dt.uint32
ALU = mybir.AluOpType
ACT = mybir.ActivationFunctionType
AX = mybir.AxisListType

P = 128
B, SQ, D, SK = 16, 64, 128, 1601
NH, DK = 16, 8
NG = 4
KS = 96
NT = -(-SK // P)
TAIL = SK - (NT - 1) * P
SKP = SK + SK % 2
CH = 4
CW = [512, 512, 512, TAIL]
NJ = 8
UNITS = CH * NJ
TOK = B * SQ
NTT = TOK // P
EPS = 1e-5
MASKED = -10000.0
MARK = -125.0 * 2.0 ** 60
MARK_TO_MASKED = 80.0 * 2.0 ** -60
CHUNK_STEPS = {0: (1, 3, 0), 1: (1, 3, 1), 2: (1, 3, 2), 3: (2, 0, 0), 4: (2, 0, 1), 5: (2, 0, 2),
               6: (2, 1, 0), 7: (2, 1, 1), 8: (2, 1, 2), 10: (2, 2, 0), 11: (2, 2, 1), 12: (2, 2, 2)}
UNIT_SLOTS = [2, 3, 3, 3, 3, 2, 4, 4, 4, 4, 0, 0, 0]
UNIT_AT = [sum(UNIT_SLOTS[:t]) for t in range(NT)]
MAX_SLOT = 10
RELOC = 2 * 6 * 16


def tile_rows(t):
    return P if t < NT - 1 else TAIL


def cross_attention(nc, io, keep):
    ou, xall, cst, ones = keep.ou, keep.x, keep.constants, keep.ones
    with ExitStack() as ctx:
        def sb(name, shape, dt=F32):
            return ctx.enter_context(nc.sbuf_tensor(name, shape, dt))

        def sem(name):
            return ctx.enter_context(nc.semaphore(name))

        kst = [sb(f"key_stack{i}", [KS + 2, NG, SKP], F32R) for i in range(2)]
        vx = sb("values", [P, 2, NT, 2 * P])
        st_hi = sb("keys_hi", [P, SK], F32R)
        st_lo = sb("keys_lo", [P, SK], F32R)
        ctxb = sb("context", [P, 2, 3, 4, D])
        ctail = sb("context_tail", [TAIL, 2, D])
        ctxT = sb("context_T", [P, 2, 512])
        probs = sb("probs", [P, 2, 1024])
        q1 = [sb(f"q_pass1_{i}", [KS, 1024], F32R) for i in range(2)]
        q2 = [sb(f"q_pass2_{i}", [KS + 2, 1024], F32R) for i in range(2)]
        qr = sb("q_roles", [P, NG, TOK])
        mraw = sb("mask_raw", [P, SK], I32)
        a1 = [sb(f"mark_pass1_{i}", [P, SK], BF16) for i in range(2)]
        a2 = [sb(f"mark_pass2_{i}", [SQ, SK], BF16) for i in range(2)]
        sjunk = sb("masked_scores_junk", [P, 2, 512], BF16)
        mx = sb("chunk_max", [P, 2, NJ, CH])
        mxr = sb("row_max", [P, NJ])
        asum = sb("mark_sum", [P, 2])
        flr = sb("max_floor", [P, 2])
        negm = sb("neg_max", [P, NJ])
        mh = sb("neg_max_hi_lo", [P, 2 * NJ])
        mrow = sb("neg_max_rows", [2 * NJ, 2, P])
        flag = sb("any_masked", [1, 2], I32)
        xn = sb("x_normed", [P, NTT, D])
        ajunk = xn[:, :, :].rearrange("p t d -> p (t d)").bitcast(BF16)[:, 0:SK]
        xnT = sb("x_normed_T", [P, TOK])
        bst = sb("ln_stats", [P, NTT, 6])
        bag = sb("ln_mean_var", [P, NTT, 2])
        rstd = sb("ln_rstd", [P, NTT])
        ident = cst[:, 0:P]
        bd = cst[0:KS, P:P + NG]
        eps = cst[:, P + NG:P + NG + 1]
        wq = sb("w_q", [P, P])
        wqr = sb("w_q_roles", [P, NG, 3, 32])
        wk = sb("w_k", [P, P])
        wv = sb("w_v", [P, P])
        bqr = sb("b_q_roles", [KS, NG])
        bk = sb("b_k", [P, 1])
        mrhs = sb("mark_rhs", [SQ, 3, 8, SQ], BF16)
        warm = sb("warm", [P, 2])

        s2 = [ctx.enter_context(nc.psum_tensor(f"scores{i}", [P, 1024], F32)) for i in range(2)]
        s1 = [ctx.enter_context(nc.psum_tensor(f"scores_rows{i}", [P, 512], F32)) for i in range(2)]
        po = ctx.enter_context(nc.psum_tensor("out_acc", [P, 512], F32))
        pc = ctx.enter_context(nc.psum_tensor("chunk", [P, 512], F32))

        const_landed = sem("const_landed")
        x_landed = sem("x_landed")
        w_landed = sem("w_landed")
        kvw_landed = sem("kvw_landed")
        ctx_landed = [sem(f"ctx_landed{i}") for i in range(2)]
        mask_landed = sem("mask_landed")
        mark_ready = sem("mark_ready")
        mark2_ready = sem("mark2_ready")
        q1_ready = sem("q1_ready")
        q2_ready = sem("q2_ready")
        reloc_landed = [sem(f"reloc_landed{i}") for i in range(2)]
        negmax_landed = sem("negmax_landed")
        tp_ready = sem("tp_ready")
        ctxT_copied = sem("ctxT_copied")
        kproj_ready = sem("kproj_ready")
        khi_ready = sem("khi_ready")
        klo_ready = sem("klo_ready")
        vproj_ready = sem("vproj_ready")
        v_copied = sem("v_copied")
        unit_ready = sem("unit_ready")
        unit_done = sem("unit_done")
        marksum_ready = sem("marksum_ready")
        max_chain = sem("max_chain")
        negmax_ready = sem("negmax_ready")
        negmax_rows = sem("negmax_rows")
        negmax_copied = sem("negmax_copied")
        scores_ready = sem("scores_ready")
        exp_done = sem("exp_done")
        pv_done = sem("pv_done")
        out_bank_free = sem("out_bank_free")
        init_done = sem("init_done")
        ones_ready = sem("ones_ready")
        dve_seq = sem("dve_seq")
        var_ready = sem("var_ready")
        std_ready = sem("std_ready")
        xn_ready = sem("xn_ready")
        xnT_ready = sem("xnT_ready")
        xnT_copied = sem("xnT_copied")
        qp_ready = sem("qp_ready")
        qr_ready = sem("qr_ready")
        qhi_ready = sem("qhi_ready")
        bq_scaled = sem("bq_scaled")
        pool_passed = sem("pool_passed")
        pe_passed = sem("pe_passed")
        dve_passed = sem("dve_passed")

        block = ctx.enter_context(nc.Block())

        def one(ap, b):
            return ap[b] if isinstance(b, int) else ap[bass.ds(b, 1)].squeeze(0)

        @block.sync
        def _(sp):
            sp.dma_start(xall[:, :, :], io["x"].rearrange("b s d -> (b s) d").rearrange("(t p) d -> p t d", p=P)).then_inc(x_landed, 16)
            sp.dma_start(cst[:, :], io["constants"]).then_inc(const_landed, 16)

            def load_ctx(b, par):
                src = one(io["ctx"], b)
                if not (isinstance(b, int) and b < 2):
                    sp.wait_ge(tp_ready, CH * (b - 1))
                sp.dma_start(ctxb[:, par, :, :, :].rearrange("p c j d -> p c (j d)"),
                             src[0:3 * 512, :].rearrange("(c p j) d -> p c (j d)", p=P, j=4)).then_inc(ctx_landed[par], 16)
                sp.dma_start(ctail[:, par, :], src[3 * 512:SK, :]).then_inc(ctx_landed[par], 16)

            def load_mask(b):
                if not (isinstance(b, int) and b < 1):
                    sp.wait_ge(mark_ready, b)
                for r in range(2):
                    sp.dma_start(mraw[SQ * r:SQ * r + SQ, :], one(io["mask"], b)).then_inc(mask_landed, 16)

            def relocate(b, par, half, roles=(0, 1, 2)):
                sp.wait_ge(klo_ready, CH * b + 2 * (half + 1))
                lo, hi = (0, 1024) if half == 0 else (1024, SK)
                if half == 0 and not (isinstance(b, int) and b < 2):
                    sp.wait_ge(scores_ready, NT * (b - 2) + 8)
                for role in roles:
                    src = (st_hi, st_lo, st_hi)[role]
                    for g in range(NG):
                        sp.dma_start(kst[par][32 * role:32 * role + 32, g, lo:hi].bitcast(F32),
                                     src[32 * g:32 * g + 32, lo:hi].bitcast(F32)).then_inc(reloc_landed[half], 16)

            def send_negmax(b, par):
                sp.wait_ge(negmax_copied, b + 1)
                sp.wait_ge(q2_ready, b + 1)
                for r in range(2):
                    sp.dma_start(q2[par][KS + r:KS + r + 1, :].rearrange("p (k c) -> p k c", c=P).bitcast(F32),
                                 mrow[NJ * r:NJ * r + NJ, par, :]).then_inc(negmax_landed, 16)

            load_ctx(0, 0)
            sp.dma_start(wk[:, :], io["Wk"]).then_inc(kvw_landed, 16)
            sp.dma_start(wv[:, :], io["Wv"]).then_inc(kvw_landed, 16)
            sp.dma_start(bk[:, :], io["bk"].rearrange("(p a) -> p a", a=1)).then_inc(kvw_landed, 16)
            sp.dma_start(wq[:, :], io["Wq"]).then_inc(w_landed, 16)
            with nc.allow_non_contiguous_dma(reason="a bias of 128 values"):
                for r in range(3):
                    sp.dma_start(bqr[32 * r:32 * r + 32, :], io["bq"].rearrange("(g c) -> c g", c=32)).then_inc(w_landed, 16)
            load_mask(0)
            load_ctx(1, 1)
            relocate(0, 0, 0)
            relocate(0, 0, 1)
            load_mask(1)
            relocate(1, 1, 0, (0, 1))
            send_negmax(0, 0)
            relocate(1, 1, 0, (2,))

            def batch(b, par, chunks, pass1):
                if chunks:
                    load_ctx(b + 2, par)
                    load_mask(b + 2)
                if pass1:
                    relocate(b + 1, 1 - par, 1)
                if chunks:
                    relocate(b + 2, par, 0, (0, 1))
                if pass1:
                    send_negmax(b + 1, 1 - par)
                if chunks:
                    relocate(b + 2, par, 0, (2,))

            with sp.Fori(0, B // 2 - 1) as i:
                batch(2 * i, 0, True, True)
                batch(2 * i + 1, 1, True, True)
            batch(B - 2, 0, False, True)

        @block.gpsimd
        def _(pool):
            for k in range(2):
                pool.memset(kst[k][KS:KS + 2, :, :].bitcast(F32), 1.0).then_inc(ones_ready, 1)
            pool.wait_ge(ones_ready, 2)
            pool.memset(vx[:, 1, :, :], 0.0).then_inc(ones_ready, 1)
            pool.wait_ge(ones_ready, 3)
            for k in range(2):
                pool.memset(kst[k][0:KS, :, SK:SKP].bitcast(F32), 0.0).then_inc(ones_ready, 1)
            pool.memset(vx[:, 1, :, :].rearrange("p t (h e) -> p (t h) e", e=16)[:, :, DK:DK + 1], 1.0).then_inc(init_done, 1)
            pool.wait_ge(ones_ready, 5)

            def spread(dst, b, ready):
                out = dst[0:KS, :].rearrange("p (g h q) -> p g h q", g=NG, h=4)
                for h in range(4):
                    op = pool.tensor_tensor(out[:, :, h, :], qr[0:KS, :, b * SQ:(b + 1) * SQ] if isinstance(b, int)
                                            else qr[0:KS, :, bass.ds(b * SQ, SQ)],
                                            bd[:, h:h + 1].unsqueeze(1).to_broadcast([KS, NG, SQ]), ALU.mult)
                op.then_inc(ready, 1)

            def marks(b, par):
                if not (isinstance(b, int) and b < 2):
                    pool.wait_ge(unit_done, UNITS * (b - 1))
                pool.wait_ge(mask_landed, 32 * (b + 1))
                pool.sem_inc(pool_passed, 1)
                pool.tensor_scalar(a1[par][:, :], mraw[:, :], 0, MARK, ALU.is_le, ALU.mult).then_inc(mark_ready, 1)

            def marks2(b, par):
                pool.wait_ge(mark_ready, b + 1)
                pool.sem_inc(pool_passed, 1)
                pool.tensor_copy(a2[par][:, :], a1[par][0:SQ, :]).then_inc(mark2_ready, 1)

            marks(0, 0)
            pool.wait_ge(const_landed, 16)
            pool.wait_ge(qr_ready, NG)
            spread(q1[0], 0, q1_ready)
            spread(q2[0], 0, q2_ready)
            marks2(0, 0)
            spread(q1[1], 1, q1_ready)
            marks(1, 1)
            spread(q2[1], 1, q2_ready)
            marks2(1, 1)

            def batch(b, par):
                pool.wait_ge(unit_ready, UNITS * (b + 1))
                pool.sem_inc(pool_passed, 1)
                spread(q1[par], b + 2, q1_ready)
                marks(b + 2, par)
                pool.wait_ge(scores_ready, NT * (b + 1))
                pool.sem_inc(pool_passed, 1)
                spread(q2[par], b + 2, q2_ready)
                marks2(b + 2, par)

            with pool.Fori(0, B // 2 - 1) as i:
                batch(2 * i, 0)
                batch(2 * i + 1, 1)

        @block.scalar
        def _(act):
            act.wait_ge(const_landed, 16)
            act.wait_ge(var_ready, 1)
            nc.scalar.activation(rstd[:, :], bag[:, :, 1], ACT.Sqrt, bias=eps).then_inc(std_ready, 1)
            for k in range(2):
                nc.scalar.activation(warm[:, k:k + 1], eps, ACT.Exp).then_inc(exp_done, 1)

            def chunk_copy(b, par, c, step, pc=pc):
                q = CH * b + c
                w = CW[c]
                if step == 0:
                    act.wait_ge(tp_ready, q + 1)
                    if c < 3:
                        nc.scalar.activation(ctxT[:, c % 2, :].rearrange("d (p j) -> d j p", j=4),
                                             pc[:, :].rearrange("d (j p) -> d j p", j=4), ACT.Copy).then_inc(ctxT_copied, 1)
                    else:
                        nc.scalar.activation(ctxT[:, c % 2, 0:w], pc[:, 0:w], ACT.Copy).then_inc(ctxT_copied, 1)
                elif step == 1:
                    act.wait_ge(kproj_ready, q + 1)
                    if not (isinstance(b, int) and b < 1):
                        act.wait_ge(reloc_landed[c // 2], RELOC * b)
                    nc.scalar.activation(st_hi[:, 512 * c:512 * c + w], pc[:, 0:w], ACT.Identity, bias=bk[:, 0:1]).then_inc(khi_ready, 1)
                else:
                    act.wait_ge(vproj_ready, q + 1)
                    if not (isinstance(b, int) and b < 2):
                        act.wait_ge(pv_done, NT * (b - 2) + min(4 * c + 3, NT - 1) + 3)
                    n = 4 if c < 3 else 1
                    r = P if c < 3 else TAIL
                    nc.scalar.activation(vx[0:r, par, 4 * c:4 * c + n, :].rearrange("p t (h e) -> p t h e", e=16)[:, :, :, 0:DK],
                                         pc[0:r, 0:n * P].rearrange("p (t h d) -> p t h d", t=n, d=DK), ACT.Copy).then_inc(v_copied, 1)

            def exp(b, par, t):
                s = NT * b + t
                k = (NT * par + t) % 2
                r = tile_rows(t)
                act.wait_ge(scores_ready, s + 1)
                act.wait_ge(pv_done, s + 1)
                nc.scalar.activation(probs[0:r, k, :], s2[k][0:r, :], ACT.Exp).then_inc(exp_done, 1)

            def mark_sum(b, par):
                act.wait_ge(mark_ready, b + 1)
                nc.scalar.activation(ajunk[:, :], a1[par][:, :], ACT.Identity, accum_out=asum[:, par:par + 1]).then_inc(marksum_ready, 1)

            def query_hi(g):
                act.wait_ge(qp_ready, g + 1)
                nc.scalar.activation(qr[0:KS, g, :].bitcast(F32R), s2[(g + 1) % 2][0:KS, :], ACT.Identity,
                                     bias=bqr[:, g:g + 1]).then_inc(qhi_ready, 1)

            act.wait_ge(kvw_landed, 48)
            act.wait_ge(bq_scaled, 1)
            act.wait_ge(init_done, 2)
            for c in (0, 2):
                for k in (c, c + 1):
                    chunk_copy(0, 0, k, 0, (pc, po)[k % 2])
                if c == 2:
                    query_hi(0)
                    query_hi(1)
                for step in (1, 2):
                    for k in (c, c + 1):
                        chunk_copy(0, 0, k, step, (pc, po)[k % 2])
            query_hi(2)
            query_hi(3)
            act.wait_ge(xnT_ready, 1)
            mark_sum(0, 0)
            for c in range(3):
                for step in range(3):
                    chunk_copy(1, 1, c, step)

            def batch(b, par, chunks, pass1):
                for t in range(NT):
                    ahead, c, step = CHUNK_STEPS.get(t - 1, (9, 0, 0))
                    if (ahead == 1 and pass1) or (ahead == 2 and chunks):
                        chunk_copy(b + ahead, (par + ahead) % 2, c, step)
                    exp(b, par, t)
                    if t == 3 and pass1:
                        mark_sum(b + 1, 1 - par)
                if chunks:
                    ahead, c, step = CHUNK_STEPS[NT - 1]
                    chunk_copy(b + ahead, par, c, step)

            with act.Fori(0, B // 2 - 1) as i:
                batch(2 * i, 0, True, True)
                batch(2 * i + 1, 1, True, True)
            batch(B - 2, 0, False, True)
            batch(B - 1, 1, False, False)

        @block.tensor
        def _(pe):
            def turn_tokens():
                for n in range(NTT):
                    pe.wait_ge(xn_ready, n + 1)
                    last = nc.tensor.transpose(s2[0][:, P * n:P * n + P], xn[:, n, :], ident)
                last.then_inc(xnT_ready, 1)

            def query(g):
                pe.wait_ge(xnT_copied, 1)
                if g >= 2:
                    pe.wait_ge(qr_ready, g - 1)
                for n in range(2):
                    last = nc.tensor.matmul(s2[(g + 1) % 2][0:KS, 512 * n:512 * n + 512], wqr[:, g, :, :].rearrange("p r c -> p (r c)"),
                                            xnT[:, 512 * n:512 * n + 512], start=True, stop=True)
                last.then_inc(qp_ready, 1)

            def chunk(b, par, c, step, pc=pc):
                q = CH * b + c
                w = CW[c]
                if step == 0:
                    if c == 0:
                        pe.wait_ge(ctx_landed[par], 16 * (b - par) + 32)
                    if not isinstance(b, int) or b > 0:
                        pe.wait_ge(v_copied, q)
                    elif c >= 2:
                        pe.wait_ge(v_copied, c - 1)
                    for j in range(4 if c < 3 else 1):
                        last = (nc.tensor.transpose(pc[:, P * j:P * j + P], ctxb[:, par, c, j, :], ident) if c < 3 else
                                nc.tensor.transpose(pc[:, 0:TAIL], ctail[:, par, :], ident[0:TAIL, 0:TAIL]))
                    last.then_inc(tp_ready, 1)
                elif step == 1:
                    pe.wait_ge(ctxT_copied, q + 1)
                    nc.tensor.matmul(pc[:, 0:w], wk[:, :], ctxT[:, c % 2, 0:w], start=True, stop=True).then_inc(kproj_ready, 1)
                else:
                    pe.wait_ge(klo_ready, q + 1)
                    for j in range(4 if c < 3 else 1):
                        r = P if c < 3 else TAIL
                        last = nc.tensor.matmul(pc[0:r, P * j:P * j + P], ctxT[:, c % 2, P * j:P * j + r], wv[:, :], start=True, stop=True)
                    last.then_inc(vproj_ready, 1)

            def unit(b, par, k):
                c, j = divmod(k, NJ)
                u = UNITS * b + k
                if k == 0:
                    pe.wait_ge(q1_ready, b + 1)
                if k in (0, 2 * NJ):
                    pe.wait_ge(reloc_landed[c // 2], RELOC * (b + 1))
                if not (isinstance(b, int) and u < 2):
                    pe.wait_ge(unit_done, u - 1)
                w = CW[c] + CW[c] % 2
                nc.tensor.matmul(s1[k % 2][:, 0:w], q1[par][0:KS, P * j:P * j + P],
                                 kst[par][0:KS, j // 2, 512 * c:512 * c + w], start=True, stop=True).then_inc(unit_ready, 1)

            def max_rows(b, par):
                pe.wait_ge(negmax_ready, b + 1)
                nc.tensor.transpose(s1[0][0:2 * NJ, 0:P], mh[:, :], ident)
                nc.tensor.matmul(s1[0][0:1, P:P + 1], asum[:, par:par + 1], ones[:, :], start=True, stop=True).then_inc(negmax_rows, 1)

            def score_rows(par, t, p0, p1, first):
                k = (NT * par + t) % 2
                r = tile_rows(t)
                for g in range(NG):
                    last = nc.tensor.matmul(s2[k][0:r, 256 * g:256 * g + 256], kst[par][p0:p1, g, P * t:P * t + r],
                                            q2[par][p0:p1, 256 * g:256 * g + 256], start=first and g % 2 == 0, stop=True,
                                            skip_group_check=True)
                return last

            def mark_scores(par, t):
                k = (NT * par + t) % 2
                r = tile_rows(t)
                for f in range(3):
                    for n in range(2):
                        nc.tensor.matmul(s2[k][0:r, 512 * n:512 * n + 512], a2[par][:, P * t:P * t + r],
                                         mrhs[:, f, :, :].rearrange("p h q -> p (h q)"), start=False, stop=True, skip_group_check=True)

            def scores(b, par, t, masked):
                if t == 0:
                    pe.wait_ge(negmax_landed, 32 * (b + 1))
                pe.wait_ge(exp_done, NT * b + t + 1)
                with pe.If(masked > 0):
                    score_rows(par, t, 0, KS, True)
                    mark_scores(par, t)
                    score_rows(par, t, KS, KS + 2, False).then_inc(scores_ready, 1)
                with pe.Else():
                    score_rows(par, t, 0, KS + 2, True).then_inc(scores_ready, 1)

            def pv(b, par, t, half):
                s = NT * b + t
                k = (NT * par + t) % 2
                r = tile_rows(t)
                if half == 0:
                    pe.wait_ge(exp_done, s + 3)
                    if t == 0:
                        pe.wait_ge(out_bank_free, b + 1)
                for c in range(4):
                    j = 4 * half + c
                    last = nc.tensor.matmul(po[32 * c:32 * c + 32, P * half:P * half + P], vx[0:r, par, t, 32 * j:32 * j + 32],
                                            probs[0:r, k, P * j:P * j + P], start=(t == 0 and half == 0), stop=(t == NT - 1), skip_group_check=True)
                if half == 1:
                    last.then_inc(pv_done, 1)

            pe.wait_ge(const_landed, 16)
            for k in range(2):
                nc.tensor.transpose(po[:, 0:P], ident, ident).then_inc(pv_done, 1)
            pe.wait_ge(kvw_landed, 48)
            pe.wait_ge(init_done, 2)
            pe.wait_ge(ones_ready, 5)
            for c in (0, 2):
                for k in (c, c + 1):
                    chunk(0, 0, k, 0, (pc, po)[k % 2])
                if c == 2:
                    query(0)
                    query(1)
                for step in (1, 2):
                    for k in (c, c + 1):
                        chunk(0, 0, k, step, (pc, po)[k % 2])
                if c == 0:
                    turn_tokens()
            query(2)
            query(3)
            for n in range(9):
                chunk(1, 1, n // 3, n % 3)
                for k in range(4 * n, min(4 * n + 4, UNITS)):
                    unit(0, 0, k)
            max_rows(0, 0)

            def batch(b, par, chunks, pass1):
                pe.wait_ge(negmax_copied, b + 1)
                pe.wait_ge(mark2_ready, b + 1)
                pe.sem_inc(pe_passed, 1)
                masked = pe.value_load(flag[0:1, par:par + 1], min_val=0, max_val=1)
                for t in range(NT):
                    scores(b, par, t, masked)
                    fill = list(range(UNIT_AT[t], UNIT_AT[t] + UNIT_SLOTS[t])) if pass1 else []
                    for half in range(2):
                        if fill:
                            unit(b + 1, 1 - par, fill.pop(0))
                        if t > 0:
                            pv(b, par, t - 1, half)
                    if len(fill) > 1:
                        unit(b + 1, 1 - par, fill.pop(0))
                    ahead, c, step = CHUNK_STEPS.get(t, (9, 0, 0))
                    if (ahead == 1 and pass1) or (ahead == 2 and chunks):
                        chunk(b + ahead, (par + ahead) % 2, c, step)
                    for k in fill:
                        unit(b + 1, 1 - par, k)
                    if t == MAX_SLOT and pass1:
                        max_rows(b + 1, 1 - par)
                pv(b, par, NT - 1, 0)
                pv(b, par, NT - 1, 1)

            with pe.Fori(0, B // 2 - 1) as i:
                batch(2 * i, 0, True, True)
                batch(2 * i + 1, 1, True, True)
            batch(B - 2, 0, False, True)
            batch(B - 1, 1, False, False)

        @block.vector
        def _(dve):
            seq = [0]

            def link(op):
                seq[0] += 1
                op.then_inc(dve_seq, 1)
                dve.wait_ge(dve_seq, seq[0])

            link(nc.vector.memset(vx[:, 0, :, :], 0.0))
            nc.vector.memset(vx[:, 0, :, :].rearrange("p t (h e) -> p (t h) e", e=16)[:, :, DK:DK + 1], 1.0).then_inc(init_done, 1)
            nc.vector.memset(ones[:, :], 1.0)
            nc.vector.memset(sjunk[:, 0, 0:2], 0.0).then_inc(out_bank_free, 1)
            dve.wait_ge(x_landed, 16)
            for n in range(NTT):
                last = nc.vector.bn_stats(bst[:, n, :], xall[:, n, :])
            link(last)
            for n in range(NTT):
                last = nc.vector.bn_aggr(bag[:, n, :], bst[:, n, :])
            last.then_inc(var_ready, 1)
            dve.wait_ge(w_landed, 16 * 4)
            link(nc.vector.tensor_scalar(wq[:, :], wq[:, :], DK ** -0.5, None, ALU.mult))
            for r in range(3):
                nc.vector.tensor_copy(wqr[:, :, r, :], wq[:, :].rearrange("p (g c) -> p g c", c=32))
            nc.vector.tensor_scalar(bqr[:, :], bqr[:, :], DK ** -0.5, None, ALU.mult).then_inc(bq_scaled, 1)
            dve.wait_ge(bq_scaled, 1)
            dve.wait_ge(std_ready, 1)
            dve.wait_ge(var_ready, 1)
            link(nc.vector.reciprocal(rstd[:, :], rstd[:, :]))
            for n in range(NTT):
                nc.vector.tensor_scalar(xn[:, n, :], xall[:, n, :], bag[:, n, 0:1], rstd[:, n:n + 1],
                                        ALU.subtract, ALU.mult).then_inc(xn_ready, 1)
            dve.wait_ge(const_landed, 16)
            for f, w in enumerate((1.0, -1.0, MARK_TO_MASKED)):
                nc.vector.tensor_scalar(mrhs[:, f, :, :], ident[0:SQ, 0:SQ].unsqueeze(1).to_broadcast([SQ, 8, SQ]), w, None, ALU.mult)

            def query_lo(g):
                dve.wait_ge(qhi_ready, g + 1)
                nc.vector.scalar_tensor_tensor(out=qr[64:96, g, :], in0=s2[(g + 1) % 2][64:96, :], scalar=bqr[64:96, g:g + 1],
                                               in1=qr[64:96, g, :], op0=ALU.add, op1=ALU.subtract).then_inc(qr_ready, 1)

            def key_lo(b, c, pc=pc):
                q = CH * b + c
                w = CW[c]
                dve.wait_ge(khi_ready, q + 1)
                nc.vector.scalar_tensor_tensor(out=st_lo[:, 512 * c:512 * c + w], in0=pc[:, 0:w], scalar=bk[:, 0:1],
                                               in1=st_hi[:, 512 * c:512 * c + w].bitcast(F32), op0=ALU.add,
                                               op1=ALU.subtract).then_inc(klo_ready, 1)

            def unit(b, par, k):
                c, j = divmod(k, NJ)
                if k == 0:
                    dve.wait_ge(mark_ready, b + 1)
                dve.wait_ge(unit_ready, UNITS * b + k + 1)
                dve.sem_inc(dve_passed, 1)
                nc.vector.tensor_tensor_reduce(out=sjunk[:, k % 2, 0:CW[c]], in0=s1[k % 2][:, 0:CW[c]], in1=a1[par][:, 512 * c:512 * c + CW[c]],
                                               scale=1.0, scalar=-3.0e38, op0=ALU.add, op1=ALU.max,
                                               accum_out=mx[:, par, j, c:c + 1]).then_inc(unit_done, 1)

            def find_max(b, par):
                n = 5 * b

                def then(op, k):
                    op.then_inc(max_chain, 1)
                    dve.wait_ge(max_chain, n + k)

                dve.wait_ge(marksum_ready, b + 1)
                nc.vector.tensor_scalar(flr[:, 0:1], asum[:, par:par + 1], 0.0, -3.0e38, ALU.is_equal, ALU.mult).then_inc(max_chain, 1)
                dve.wait_ge(unit_done, UNITS * (b + 1))
                nc.vector.tensor_reduce(mxr[:, :], mx[:, par, :, :], axis=AX.X, op=ALU.max).then_inc(max_chain, 1)
                dve.wait_ge(max_chain, n + 2)
                then(nc.vector.tensor_scalar(flr[:, 1:2], flr[:, 0:1], MASKED, None, ALU.add), 3)
                then(nc.vector.tensor_scalar(negm[:, :], mxr[:, :], flr[:, 1:2], -1.0, ALU.max, ALU.mult), 4)
                then(nc.vector.tensor_copy(mh[:, 0:NJ].bitcast(F32R), negm[:, :]), 5)
                nc.vector.tensor_tensor(mh[:, NJ:2 * NJ].bitcast(F32R), negm[:, :], mh[:, 0:NJ], ALU.subtract).then_inc(negmax_ready, 1)

            def copy_max(b, par):
                dve.wait_ge(negmax_rows, b + 1)
                nc.vector.tensor_copy(mrow[:, par, :], s1[0][0:2 * NJ, 0:P])
                nc.vector.tensor_scalar(flag[0:1, par:par + 1], s1[0][0:1, P:P + 1], 0.0, None, ALU.is_lt).then_inc(negmax_copied, 1)

            key_lo(0, 0, pc)
            key_lo(0, 1, po)
            dve.wait_ge(xnT_ready, 1)
            nc.vector.tensor_copy(xnT[:, :], s2[0][:, :]).then_inc(xnT_copied, 1)
            query_lo(0)
            query_lo(1)
            key_lo(0, 2, pc)
            key_lo(0, 3, po)
            query_lo(2)
            query_lo(3)
            for n in range(9):
                if n % 3 == 2:
                    key_lo(1, n // 3)
                for k in range(4 * n, min(4 * n + 4, UNITS)):
                    unit(0, 0, k)
            find_max(0, 0)
            copy_max(0, 0)

            def batch(pair, par, chunks, pass1):
                b = 2 * pair + par
                for t in range(NT):
                    fill = list(range(UNIT_AT[t], UNIT_AT[t] + UNIT_SLOTS[t])) if pass1 else []
                    if fill:
                        unit(b + 1, 1 - par, fill.pop(0))
                    ahead, c, step = CHUNK_STEPS.get(t - 1, (9, 0, 0))
                    if step == 1 and ((ahead == 1 and pass1) or (ahead == 2 and chunks)):
                        key_lo(b + ahead, c)
                    for k in fill:
                        unit(b + 1, 1 - par, k)
                    if t == MAX_SLOT - 1 and pass1:
                        find_max(b + 1, 1 - par)
                    if t == MAX_SLOT + 1 and pass1:
                        copy_max(b + 1, 1 - par)
                dve.wait_ge(pv_done, NT * (b + 1) + 2)
                nc.vector.tensor_copy(ou[:, pair, :, par, :] if isinstance(b, int) else ou[:, bass.ds(pair, 1), :, par, :].squeeze(1),
                                      po[:, 0:2 * P].rearrange("p (k q) -> p k q", q=SQ)).then_inc(out_bank_free, 1)

            with dve.Fori(0, B // 2 - 1) as i:
                batch(i, 0, True, True)
                batch(i, 1, True, True)
            batch(B // 2 - 1, 0, False, True)
            batch(B // 2 - 1, 1, False, False)


KVH, DH = 4, 64
GA = 4
NE, NHID = 8, 512
HC = NHID // P
NBKT = 32
FAR = -1.0e30


def layer_norm_stats(dve, seq_link, stats, aggr, x):
    for n in range(NTT):
        last = dve.bn_stats(stats[:, n, :], x[:, n, :])
    seq_link(last)
    for n in range(NTT):
        last = dve.bn_aggr(aggr[:, n, :], stats[:, n, :])
    return last


def self_attention(nc, io, keep):
    ou, x, cst = keep.ou, keep.x, keep.constants
    ident = cst[:, 0:P]
    eps = cst[:, P + NG:P + NG + 1]
    with ExitStack() as ctx:
        def sb(name, shape, dt=F32):
            return ctx.enter_context(nc.sbuf_tensor(name, shape, dt))

        def sem(name):
            return ctx.enter_context(nc.semaphore(name))

        wo1 = sb("w_out1", [P, P])
        bvb = sb("b_v_rows", [P, P])
        bob = sb("b_out_rows", [P, P])
        waq = sb("w_attn_q", [P, GA, 2, P])
        wak = sb("w_attn_k", [P, GA, 2, P])
        wav = sb("w_attn_v", [P, GA, 2, P])
        wao = sb("w_attn_out", [P, GA, 2 * P])
        wsum = sb("w_group_sums", [P, 4, 2, P])
        wT = sb("w_attn_T", [P, 4, 2 * P])
        rb = sb("rel_bias", [NBKT, GA, KVH])
        rbm = sb("rel_bias_mean", [NBKT, KVH])
        oh = sb("bucket_onehot", [NBKT, 2 * SQ - 1])
        bias = sb("score_bias", [P, KVH, P])
        rd = sb("out_rdenom", [P, 2, 2, 2, 4])
        on = sb("out_norm", [P, NTT, P])
        oT = sb("out_T", [P, 2, P])
        bst = sb("ln_stats_b", [P, NTT, 6])
        bag = sb("ln_aggr_b", [P, NTT, 2])
        rstd = sb("ln_rstd_b", [P, NTT])
        xn = sb("x_normed_b", [P, NTT, D])
        xnT = sb("x_normed_T_b", [P, TOK])
        qT = sb("attn_q_T", [P, 2, TOK])
        kT = sb("attn_k_T", [P, 2, TOK])
        va = sb("attn_v", [P, NTT, 2 * P])
        sc = sb("attn_scores", [P, NTT, KVH, P])
        ngm = sb("attn_negmax", [P, NTT, KVH])
        pr = sb("attn_probs", [P, NTT, KVH, P])
        den = sb("attn_denom", [P, NTT, KVH])
        prT = sb("attn_probs_T", [P, 2, KVH, P])
        ao = sb("attn_out", [P, 2, 2 * P])
        aoT = sb("attn_out_T", [P, 2, 2 * P])
        ps = [ctx.enter_context(nc.psum_tensor(f"bank{i}", [P, 512], F32)) for i in range(8)]

        w_landed = sem("attn_w_landed")
        dve_seq = sem("attn_dve_seq")
        sums_ready = sem("group_sums_ready")
        wT_ready = sem("wT_ready")
        wT_copied = sem("wT_copied")
        bias_ready = sem("bias_ready")
        o_turned = sem("o_turned")
        o_normed = sem("o_normed")
        oT_ready = sem("oT_ready")
        oT_copied = sem("oT_copied")
        y1_ready = sem("y1_ready")
        x1_ready = sem("x1_ready")
        var_ready = sem("attn_var_ready")
        std_ready = sem("attn_std_ready")
        xn_ready = sem("attn_xn_ready")
        xnT_ready = sem("attn_xnT_ready")
        xnT_copied = sem("attn_xnT_copied")
        proj_ready = sem("attn_proj_ready")
        proj_copied = sem("attn_proj_copied")
        v_ready = sem("attn_v_ready")
        v_copied = sem("attn_v_copied")
        s_ready = sem("attn_s_ready")
        s_biased = sem("attn_s_biased")
        max_ready = sem("attn_max_ready")
        e_ready = sem("attn_e_ready")
        eT_ready = sem("attn_eT_ready")
        eT_copied = sem("attn_eT_copied")
        ao_ready = sem("attn_ao_ready")
        ao_normed = sem("attn_ao_normed")
        aoT_ready = sem("attn_aoT_ready")
        aoT_copied = sem("attn_aoT_copied")
        y2_ready = sem("y2_ready")
        block = ctx.enter_context(nc.Block())

        @block.sync
        def _(sp):
            n = 0
            for t, src in ((waq, io["aWq"]), (wak, io["aWk"]), (wav, io["aWv"])):
                sp.dma_start(t[:, :, :, :].rearrange("r g h m -> r (g h) m"), src.rearrange("(b r) m -> r b m", r=P)).then_inc(w_landed, 16)
            sp.dma_start(wao[:, :, :].rearrange("n g c -> n (g c)"), io["aWo"]).then_inc(w_landed, 16)
            sp.dma_start(wo1[:, :], io["Wo"]).then_inc(w_landed, 16)
            sp.dma_start(bvb[:, :], io["bv"].unsqueeze(0).to_broadcast([P, P])).then_inc(w_landed, 16)
            sp.dma_start(bob[:, :], io["bo"].unsqueeze(0).to_broadcast([P, P])).then_inc(w_landed, 16)
            sp.dma_start(rb[:, :, :].rearrange("b g h -> b (g h)"), io["rel_bias"]).then_inc(w_landed, 16)
            sp.dma_start(oh[:, :], io["bucket_onehot"]).then_inc(w_landed, 16)

        @block.scalar
        def _(act):
            act.wait_ge(wT_ready, 1)
            for k in range(4):
                op = nc.scalar.activation(wT[:, k, :], ps[k // 2][:, 256 * (k % 2):256 * (k % 2) + 256], ACT.Copy,
                                          scale=0.25 if k in (1, 2) else 1.0)
            op.then_inc(wT_copied, 1)
            for n in range(NTT):
                act.wait_ge(oT_ready, n + 1)
                nc.scalar.activation(oT[:, n % 2, :], ps[5][:, P * (n % 2):P * (n % 2) + P], ACT.Copy).then_inc(oT_copied, 1)
            act.wait_ge(var_ready, 1)
            nc.scalar.activation(rstd[:, :], bag[:, :, 1], ACT.Sqrt, bias=eps).then_inc(std_ready, 1)
            for k in range(8):
                act.wait_ge(proj_ready, k + 1)
                dst = (qT, kT)[k // 4]
                nc.scalar.activation(dst[:, k // 2 % 2, 512 * (k % 2):512 * (k % 2) + 512], ps[k % 2][:, :], ACT.Copy).then_inc(proj_copied, 1)
            for n in range(NTT):
                act.wait_ge(max_ready, n + 1)
                for h in range(KVH):
                    op = nc.scalar.activation(pr[:, n, h, :], sc[:, n, h, :], ACT.Exp, bias=ngm[:, n, h:h + 1],
                                              accum_out=den[:, n, h:h + 1])
                op.then_inc(e_ready, 1)
            for n in range(NTT):
                act.wait_ge(eT_ready, n + 1)
                nc.scalar.activation(prT[:, n % 2, :, :].rearrange("p h k -> p (h k)"), ps[n % 2][:, :], ACT.Copy).then_inc(eT_copied, 1)
                act.wait_ge(aoT_ready, n + 1)
                nc.scalar.activation(aoT[:, n % 2, :], ps[4][:, 256 * (n % 2):256 * (n % 2) + 256], ACT.Copy).then_inc(aoT_copied, 1)

        @block.tensor
        def _(pe):
            pe.wait_ge(sums_ready, 1)
            for k in range(4):
                for h in range(2):
                    last = nc.tensor.transpose(ps[k // 2][:, 256 * (k % 2) + P * h:256 * (k % 2) + P * h + P], wsum[:, k, h, :], ident)
            last.then_inc(wT_ready, 1)
            for k in range(SQ):
                last = nc.tensor.matmul(ps[2][0:SQ, KVH * k:KVH * k + KVH], oh[:, SQ - 1 - k:2 * SQ - 1 - k], rbm[:, :], start=True, stop=True)
                last = nc.tensor.matmul(ps[2][SQ:P, KVH * k:KVH * k + KVH], oh[:, SQ - 1 - k:2 * SQ - 1 - k], rbm[:, :], start=True, stop=True)
            last.then_inc(bias_ready, 1)
            def turn(n):
                if n >= 2:
                    pe.wait_ge(o_normed, n - 1)
                for k in range(4):
                    last = nc.tensor.transpose(ps[3 + n % 2][:, P * k:P * k + P], ou[:, n, k, :, :].rearrange("p b q -> p (b q)"), ident)
                last.then_inc(o_turned, 1)

            turn(0)
            for n in range(NTT):
                if n + 1 < NTT:
                    turn(n + 1)
                pe.wait_ge(o_normed, n + 1)
                if n >= 2:
                    pe.wait_ge(oT_copied, n - 1)
                nc.tensor.transpose(ps[5][:, P * (n % 2):P * (n % 2) + P], on[:, n, :], ident).then_inc(oT_ready, 1)
                pe.wait_ge(oT_copied, n + 1)
                if n >= 2:
                    pe.wait_ge(x1_ready, n - 1)
                nc.tensor.matmul(ps[6 + n % 2][:, 0:P], oT[:, n % 2, :], wo1[:, :], start=True, stop=True).then_inc(y1_ready, 1)
            for n in range(NTT):
                pe.wait_ge(xn_ready, n + 1)
                last = nc.tensor.transpose(ps[3 + n // 4][:, P * (n % 4):P * (n % 4) + P], xn[:, n, :], ident)
            last.then_inc(xnT_ready, 1)
            pe.wait_ge(xnT_copied, 1)
            pe.wait_ge(wT_copied, 1)
            for k in range(8):
                if k >= 2:
                    pe.wait_ge(proj_copied, k - 1)
                w, hp, th = k // 4, k // 2 % 2, k % 2
                nc.tensor.matmul(ps[k % 2][:, :], wT[:, w, P * hp:P * hp + P], xnT[:, 512 * th:512 * th + 512], start=True, stop=True).then_inc(proj_ready, 1)
            for n in range(NTT):
                if n >= 2:
                    pe.wait_ge(v_copied, n - 1)
                nc.tensor.matmul(ps[6 + n % 2][:, 0:256], xnT[:, P * n:P * n + P], wT[:, 2, :], start=True, stop=True).then_inc(v_ready, 1)
            pe.wait_ge(proj_copied, 8)
            for n in range(NTT):
                if n >= 2:
                    pe.wait_ge(s_biased, n - 1)
                for h in range(KVH):
                    r = DH * (h % 2)
                    last = nc.tensor.matmul(ps[2 + 2 * (n % 2) + h % 2][:, P * (h // 2):P * (h // 2) + P], qT[r:r + DH, h // 2, P * n:P * n + P],
                                            kT[r:r + DH, h // 2, P * n:P * n + P], start=True, stop=True)
                last.then_inc(s_ready, 1)
            def turn_probs(n):
                pe.wait_ge(e_ready, n + 1)
                if n >= 2:
                    pe.wait_ge(eT_copied, n - 1)
                for h in range(KVH):
                    last = nc.tensor.transpose(ps[n % 2][:, P * h:P * h + P], pr[:, n, h, :], ident)
                last.then_inc(eT_ready, 1)

            pe.wait_ge(v_copied, NTT)
            pe.wait_ge(s_biased, NTT)
            turn_probs(0)
            for n in range(NTT):
                if n + 1 < NTT:
                    turn_probs(n + 1)
                pe.wait_ge(eT_copied, n + 1)
                if n >= 2:
                    pe.wait_ge(ao_normed, n - 1)
                for h in range(KVH):
                    last = nc.tensor.matmul(ps[5 + n % 2][:, DH * h:DH * h + DH], prT[:, n % 2, h, :], va[:, n, DH * h:DH * h + DH], start=True, stop=True)
                last.then_inc(ao_ready, 1)
                pe.wait_ge(ao_normed, n + 1)
                for h in range(2):
                    last = nc.tensor.transpose(ps[4][:, 256 * (n % 2) + P * h:256 * (n % 2) + P * h + P], ao[:, n % 2, P * h:P * h + P], ident)
                last.then_inc(aoT_ready, 1)
                pe.wait_ge(aoT_copied, n + 1)
                for h in range(2):
                    last = nc.tensor.matmul(ps[7][:, P * (n % 4):P * (n % 4) + P], aoT[:, n % 2, P * h:P * h + P], wT[:, 3, P * h:P * h + P],
                                            start=(h == 0), stop=(h == 1))
                last.then_inc(y2_ready, 1)
                pe.wait_ge(keep.x2_ready, n + 1)

        @block.vector
        def _(dve):
            seq = [0]

            def link(op):
                seq[0] += 1
                op.then_inc(dve_seq, 1)
                dve.wait_ge(dve_seq, seq[0])

            dve.wait_ge(w_landed, 16 * 9)
            for k, w in enumerate((waq, wak, wav)):
                nc.vector.tensor_reduce(wsum[:, k, :, :], w[:, :, :, :].rearrange("r g h m -> r h m g"), axis=AX.X, op=ALU.add)
            nc.vector.tensor_reduce(wsum[:, 3, :, :].rearrange("n h c -> n (h c)"), wao[:, :, :].rearrange("n g c -> n c g"), axis=AX.X, op=ALU.add)
            link(nc.vector.tensor_reduce(rbm[:, :], rb[:, :, :].rearrange("b g h -> b h g"), axis=AX.X, op=ALU.add))
            nc.vector.tensor_scalar(rbm[:, :], rbm[:, :], 0.25, None, ALU.mult).then_inc(sums_ready, 1)
            link(nc.vector.memset(bias[:, :, :], FAR))
            for n in range(NTT):
                op = nc.vector.tensor_tensor(x[:, n, :], x[:, n, :], bob[:, :], ALU.add)
            link(op)
            dve.wait_ge(bias_ready, 1)
            for a in range(2):
                nc.vector.tensor_copy(bias[64 * a:64 * a + 64, :, 64 * a:64 * a + 64],
                                      ps[2][64 * a:64 * a + 64, 0:256].rearrange("q (k h) -> q h k", h=KVH))

            def normalise(n):
                dve.wait_ge(o_turned, n + 1)
                bank = ps[3 + n % 2][:, :].rearrange("p (a s c e) -> p a s c e", a=2, s=2, c=4)
                for s in range(2):
                    op = nc.vector.reciprocal(rd[:, n % 2, s, :, :], bank[:, :, s, :, 16 * s + DK])
                link(op)
                for s in range(2):
                    op = nc.vector.tensor_tensor(on[:, n, :].rearrange("p (a c s d) -> p a c s d", a=2, c=4, s=2)[:, :, :, s, :],
                                                 bank[:, :, s, :, 16 * s:16 * s + DK],
                                                 rd[:, n % 2, s, :, :].unsqueeze(3).to_broadcast([P, 2, 4, DK]), ALU.mult)
                link(op)
                nc.vector.tensor_tensor(on[:, n, :], on[:, n, :], bvb[:, :], ALU.add).then_inc(o_normed, 1)

            normalise(0)
            for n in range(NTT):
                if n + 1 < NTT:
                    normalise(n + 1)
                dve.wait_ge(y1_ready, n + 1)
                nc.vector.tensor_tensor(x[:, n, :], x[:, n, :], ps[6 + n % 2][:, 0:P], ALU.add).then_inc(x1_ready, 1)
            dve.wait_ge(x1_ready, NTT)
            layer_norm_stats(nc.vector, link, bst, bag, x).then_inc(var_ready, 1)
            dve.wait_ge(std_ready, 1)
            link(nc.vector.reciprocal(rstd[:, :], rstd[:, :]))
            for n in range(NTT):
                nc.vector.tensor_scalar(xn[:, n, :], x[:, n, :], bag[:, n, 0:1], rstd[:, n:n + 1], ALU.subtract, ALU.mult).then_inc(xn_ready, 1)
            dve.wait_ge(xnT_ready, 1)
            for k in range(2):
                op = nc.vector.tensor_copy(xnT[:, 512 * k:512 * k + 512], ps[3 + k][:, :])
            op.then_inc(xnT_copied, 1)
            for n in range(NTT):
                dve.wait_ge(v_ready, n + 1)
                nc.vector.tensor_copy(va[:, n, :], ps[6 + n % 2][:, 0:256]).then_inc(v_copied, 1)
            for n in range(NTT):
                dve.wait_ge(s_ready, n + 1)
                for r in range(2):
                    op = nc.vector.tensor_tensor(sc[:, n, r::2, :], ps[2 + 2 * (n % 2) + r][:, 0:2 * P].rearrange("p (h k) -> p h k", h=2),
                                                 bias[:, r::2, :], ALU.add)
                op.then_inc(s_biased, 1)
                dve.wait_ge(s_biased, n + 1)
                nc.vector.tensor_reduce(ngm[:, n, :], sc[:, n, :, :], axis=AX.X, op=ALU.max, negate=True).then_inc(max_ready, 1)
            for n in range(NTT):
                dve.wait_ge(e_ready, n + 1)
                link(nc.vector.reciprocal(den[:, n, :], den[:, n, :]))
                dve.wait_ge(ao_ready, n + 1)
                nc.vector.tensor_tensor(ao[:, n % 2, :].rearrange("p (h d) -> p h d", h=KVH), ps[5 + n % 2][:, 0:256].rearrange("p (h d) -> p h d", h=KVH),
                                        den[:, n, :].unsqueeze(2).to_broadcast([P, KVH, DH]), ALU.mult).then_inc(ao_normed, 1)
                dve.wait_ge(y2_ready, n + 1)
                nc.vector.tensor_tensor(x[:, n, :], x[:, n, :], ps[7][:, P * (n % 4):P * (n % 4) + P], ALU.add).then_inc(keep.x2_ready, 1)


def experts(nc, io, keep):
    x, cst = keep.x, keep.constants
    ident = cst[:, 0:P]
    eps = cst[:, P + NG:P + NG + 1]
    with ExitStack() as ctx:
        def sb(name, shape, dt=F32):
            return ctx.enter_context(nc.sbuf_tensor(name, shape, dt))

        def sem(name):
            return ctx.enter_context(nc.semaphore(name))

        w1 = sb("w1", [P, 2, NHID])
        w2 = sb("w2", [P, 2, HC, D])
        b1r = sb("b1_rows", [NE * HC, P])
        b1 = sb("b1_cols", [P, NE * HC])
        b2 = sb("b2", [NE, D])
        rw = sb("router_w", [P, NE])
        rbb = sb("router_b_rows", [P, NE])
        bst = sb("ln_stats_c", [P, NTT, 6])
        bag = sb("ln_aggr_c", [P, NTT, 2])
        rstd = sb("ln_rstd_c", [P, NTT])
        xn = sb("x_normed_c", [P, NTT, D])
        xnT = sb("x_normed_T_c", [P, TOK])
        iota = sb("expert_numbers", [P, NE])
        lg = sb("logits", [P, NTT, NE])
        top = sb("top_values", [P, NTT, NE])
        idx = sb("top_indices", [P, NTT, NE], U32)
        idf = sb("top_indices_f", [P, NTT, NE])
        kp = sb("kept", [P, NTT, NE])
        eq = sb("second_kept", [P, NTT, NE])
        gs = sb("gate_sum", [P, NTT])
        gate = sb("gates", [P, NTT, NE])
        gT = sb("gates_T", [NE, TOK])
        hT = sb("hidden", [P, 2, HC, TOK])
        ps = [ctx.enter_context(nc.psum_tensor(f"moe_bank{i}", [P, 512], F32)) for i in range(8)]

        c_landed = sem("moe_c_landed")
        w1_landed = [sem(f"w1_landed{i}") for i in range(2)]
        w2_landed = [sem(f"w2_landed{i}") for i in range(2)]
        dve_seq = sem("moe_dve_seq")
        iota_ready = sem("iota_ready")
        b1_ready = sem("b1_ready")
        b1_copied = sem("b1_copied")
        act_passed = sem("act_passed")
        var_ready = sem("moe_var_ready")
        std_ready = sem("moe_std_ready")
        xn_ready = sem("moe_xn_ready")
        xnT_ready = sem("moe_xnT_ready")
        xnT_copied = sem("moe_xnT_copied")
        logits_ready = sem("logits_ready")
        shifted = sem("logits_shifted")
        exp_ready = sem("gates_exp_ready")
        gates_ready = sem("gates_ready")
        gT_ready = sem("gT_ready")
        gT_copied = sem("gT_copied")
        b2_ready = sem("b2_ready")
        h_ready = sem("h_ready")
        h_copied = sem("h_copied")
        y_ready = sem("y_ready")
        y_added = sem("y_added")
        stored = sem("out_stored")
        block = ctx.enter_context(nc.Block())

        @block.sync
        def _(sp):
            def load(e, par):
                w1_d, w2_d = (io[k][e] if isinstance(e, int) else io[k][bass.ds(e, 1)].squeeze(0) for k in ("w1", "w2"))
                if not isinstance(e, int):
                    sp.wait_ge(h_ready, 8 * (e - 1))
                sp.dma_start(w1[:, par, :], w1_d).then_inc(w1_landed[par], 16)
                if not isinstance(e, int):
                    sp.wait_ge(y_ready, 2 * (e - 1))
                sp.dma_start(w2[:, par, :, :], w2_d.rearrange("(c p) n -> p c n", p=P)).then_inc(w2_landed[par], 16)

            sp.dma_start(rw[:, :], io["router_w"]).then_inc(c_landed, 16)
            sp.dma_start(rbb[:, :], io["router_b"].unsqueeze(0).to_broadcast([P, NE])).then_inc(c_landed, 16)
            sp.dma_start(b1r[:, :], io["b1"].rearrange("e (c p) -> (e c) p", p=P)).then_inc(c_landed, 16)
            sp.dma_start(b2[:, :], io["b2"]).then_inc(c_landed, 16)
            load(0, 0)
            load(1, 1)
            with sp.Fori(1, NE // 2) as i:
                load(2 * i, 0)
                load(2 * i + 1, 1)
            out_d = io["out"].rearrange("b s d -> (b s) d").rearrange("(t p) d -> p t d", p=P)
            for g in range(2):
                sp.wait_ge(y_added, 2 * NE + g)
                sp.dma_start(out_d[:, 4 * g:4 * g + 4, :], x[:, 4 * g:4 * g + 4, :]).then_inc(stored, 16)
            sp.wait_ge(stored, 32)

        @block.gpsimd
        def _(pool):
            pool.iota(iota[:, :], pattern=[[1, NE]], base=0, channel_multiplier=0,
                      allow_small_or_imprecise_dtypes=True).then_inc(iota_ready, 1)

        @block.scalar
        def _(act):
            act.wait_ge(var_ready, 1)
            nc.scalar.activation(rstd[:, :], bag[:, :, 1], ACT.Sqrt, bias=eps).then_inc(std_ready, 1)
            act.wait_ge(b1_ready, 1)
            nc.scalar.activation(b1[:, :], ps[4][:, 0:NE * HC], ACT.Copy).then_inc(b1_copied, 1)
            act.wait_ge(shifted, 1)
            nc.scalar.activation(gate[:, :, :], lg[:, :, :], ACT.Exp).then_inc(exp_ready, 1)
            act.wait_ge(b1_copied, 1)

            def relu(e, par):
                for k in range(8):
                    c, th = divmod(k, 2)
                    col = b1[:, HC * e + c:HC * e + c + 1] if isinstance(e, int) else b1[:, bass.ds(HC * e + c, 1)]
                    if k == 0 and not (isinstance(e, int) and e < 2):
                        act.wait_ge(y_ready, 2 * (e - 1))
                    act.wait_ge(h_ready, 8 * e + k + 1)
                    act.sem_inc(act_passed, 1)
                    nc.scalar.activation(hT[:, par, c, 512 * th:512 * th + 512], ps[k % 4][:, :], ACT.Relu, bias=col).then_inc(h_copied, 1)

            relu(0, 0)
            relu(1, 1)
            with act.Fori(1, NE // 2) as i:
                relu(2 * i, 0)
                relu(2 * i + 1, 1)

        @block.tensor
        def _(pe):
            pe.wait_ge(c_landed, 64)
            nc.tensor.transpose(ps[4][:, 0:NE * HC], b1r[:, :], ident[0:NE * HC, 0:NE * HC]).then_inc(b1_ready, 1)
            for n in range(NTT):
                pe.wait_ge(xn_ready, n + 1)
                last = nc.tensor.transpose(ps[n // 4][:, P * (n % 4):P * (n % 4) + P], xn[:, n, :], ident)
            last.then_inc(xnT_ready, 1)
            pe.wait_ge(xnT_copied, 1)
            for n in range(NTT):
                last = nc.tensor.matmul(ps[5][:, NE * n:NE * n + NE], xnT[:, P * n:P * n + P], rw[:, :], start=True, stop=True)
            last.then_inc(logits_ready, 1)

            def hidden(e, par):
                pe.wait_ge(w1_landed[par], 8 * (e - par) + 16)
                for k in range(8):
                    c, th = divmod(k, 2)
                    if not (isinstance(e, int) and 8 * e + k < 4):
                        pe.wait_ge(h_copied, 8 * e + k - 3)
                    nc.tensor.matmul(ps[k % 4][:, :], w1[:, par, P * c:P * c + P], xnT[:, 512 * th:512 * th + 512], start=True, stop=True).then_inc(h_ready, 1)

            def combine(e, par):
                pe.wait_ge(w2_landed[par], 8 * (e - par) + 16)
                pe.wait_ge(h_copied, 8 * e + 8)
                for g in range(2):
                    if not (isinstance(e, int) and e == 0):
                        pe.wait_ge(y_added, 2 * e + g)
                    for n in range(4 * g, 4 * g + 4):
                        for c in range(HC):
                            last = nc.tensor.matmul(ps[6 + g][:, P * (n % 4):P * (n % 4) + P], hT[:, par, c, P * n:P * n + P],
                                                    w2[:, par, c, :], start=(c == 0), stop=(c == HC - 1))
                    last.then_inc(y_ready, 1)

            hidden(0, 0)
            pe.wait_ge(gates_ready, 1)
            for n in range(NTT):
                last = nc.tensor.transpose(ps[4 + n // 4][0:NE, P * (n % 4):P * (n % 4) + P], gate[:, n, :], ident)
            last.then_inc(gT_ready, 1)
            pe.wait_ge(gT_copied, 1)
            for n in range(NTT):
                last = nc.tensor.matmul(ps[6 + n // 4][:, P * (n % 4):P * (n % 4) + P], gT[:, P * n:P * n + P], b2[:, :], start=True, stop=True)
            last.then_inc(b2_ready, 1)
            hidden(1, 1)
            pe.wait_ge(y_added, 1)
            combine(0, 0)
            with pe.Fori(1, NE // 2) as i:
                hidden(2 * i, 0)
                combine(2 * i - 1, 1)
                hidden(2 * i + 1, 1)
                combine(2 * i, 0)
            combine(NE - 1, 1)

        @block.vector
        def _(dve):
            seq = [0]

            def link(op):
                seq[0] += 1
                op.then_inc(dve_seq, 1)
                dve.wait_ge(dve_seq, seq[0])

            dve.wait_ge(keep.x2_ready, NTT)
            layer_norm_stats(nc.vector, link, bst, bag, x).then_inc(var_ready, 1)
            dve.wait_ge(std_ready, 1)
            link(nc.vector.reciprocal(rstd[:, :], rstd[:, :]))
            for n in range(NTT):
                nc.vector.tensor_scalar(xn[:, n, :], x[:, n, :], bag[:, n, 0:1], rstd[:, n:n + 1], ALU.subtract, ALU.mult).then_inc(xn_ready, 1)
            dve.wait_ge(xnT_ready, 1)
            for k in range(2):
                op = nc.vector.tensor_copy(xnT[:, 512 * k:512 * k + 512], ps[k][:, :])
            op.then_inc(xnT_copied, 1)
            dve.wait_ge(c_landed, 64)
            dve.wait_ge(logits_ready, 1)
            link(nc.vector.tensor_tensor(lg[:, :, :], ps[5][:, 0:NTT * NE].rearrange("p (n e) -> p n e", e=NE),
                                         rbb[:, :].unsqueeze(1).to_broadcast([P, NTT, NE]), ALU.add))
            for n in range(NTT):
                op = nc.vector.max(top[:, n, :], lg[:, n, :])
            link(op)
            for n in range(NTT):
                op = nc.vector.max_index(idx[:, n, :], top[:, n, :], lg[:, n, :])
            link(op)
            link(nc.vector.tensor_copy(idf[:, :, :], idx[:, :, :]))
            nc.vector.tensor_tensor(lg[:, :, :], lg[:, :, :], top[:, :, 0:1].to_broadcast([P, NTT, NE]), ALU.subtract).then_inc(shifted, 1)
            dve.wait_ge(iota_ready, 1)
            numbers = iota[:, :].unsqueeze(1).to_broadcast([P, NTT, NE])
            nc.vector.tensor_tensor(kp[:, :, :], numbers, idf[:, :, 0:1].to_broadcast([P, NTT, NE]), ALU.is_equal)
            link(nc.vector.tensor_tensor(eq[:, :, :], numbers, idf[:, :, 1:2].to_broadcast([P, NTT, NE]), ALU.is_equal))
            link(nc.vector.tensor_tensor(kp[:, :, :], kp[:, :, :], eq[:, :, :], ALU.add))
            dve.wait_ge(exp_ready, 1)
            link(nc.vector.tensor_tensor(gate[:, :, :], gate[:, :, :], kp[:, :, :], ALU.mult))
            link(nc.vector.tensor_reduce(gs[:, :], gate[:, :, :], axis=AX.X, op=ALU.add))
            link(nc.vector.reciprocal(gs[:, :], gs[:, :]))
            nc.vector.tensor_tensor(gate[:, :, :], gate[:, :, :], gs[:, :].unsqueeze(2).to_broadcast([P, NTT, NE]), ALU.mult).then_inc(gates_ready, 1)
            dve.wait_ge(gates_ready, 1)
            dve.wait_ge(gT_ready, 1)
            for k in range(2):
                op = nc.vector.tensor_copy(gT[:, 512 * k:512 * k + 512], ps[4 + k][0:NE, :])
            op.then_inc(gT_copied, 1)
            dve.wait_ge(b2_ready, 1)
            for k in range(2):
                op = nc.vector.tensor_tensor(x[:, 4 * k:4 * k + 4, :], x[:, 4 * k:4 * k + 4, :], ps[6 + k][:, :].rearrange("p (n d) -> p n d", n=4), ALU.add)
            op.then_inc(y_added, 1)
            dve.wait_ge(y_added, 1)

            def add(e):
                for g in range(2):
                    dve.wait_ge(y_ready, 2 * e + g + 1)
                    if not (isinstance(e, int) and e == 0):
                        dve.wait_ge(y_added, 2 * e + g)
                    for n in range(4 * g, 4 * g + 4):
                        col = gate[:, n, e:e + 1] if isinstance(e, int) else gate[:, n, bass.ds(e, 1)]
                        op = nc.vector.scalar_tensor_tensor(out=x[:, n, :], in0=ps[6 + g][:, P * (n % 4):P * (n % 4) + P], scalar=col,
                                                            in1=x[:, n, :], op0=ALU.mult, op1=ALU.add)
                    op.then_inc(y_added, 1)

            add(0)
            with dve.Fori(0, NE - 1) as i:
                add(i + 1)


class Kept:
    pass


def perceiver_program(nc, io):
    keep = Kept()
    with ExitStack() as ctx:
        keep.ou = ctx.enter_context(nc.sbuf_tensor("outs", [P, NTT, 4, 2, SQ], F32))
        keep.x = ctx.enter_context(nc.sbuf_tensor("x_tokens", [P, NTT, D], F32))
        keep.constants = ctx.enter_context(nc.sbuf_tensor("constants", [P, P + NG + 1], F32))
        keep.ones = ctx.enter_context(nc.sbuf_tensor("ones", [P, 1], F32))
        keep.x2_ready = ctx.enter_context(nc.semaphore("x2_ready"))
        cross_attention(nc, io, keep)
        self_attention(nc, io, keep)
        experts(nc, io, keep)


def shape_constants():
    import numpy as np

    table = np.zeros((P, P + NG + 1), np.float32)
    table[:, 0:P] = np.eye(P)
    for p in range(KS):
        table[p, P + p % 32 // DK] = 1.0
    table[:, P + NG] = EPS
    rel = (SQ - 1) - np.arange(2 * SQ - 1)
    dist = np.abs(rel)
    half, exact = NBKT // 2, NBKT // 4
    far = exact + (np.log(np.maximum(dist, 1).astype(np.float32) / np.float32(exact)) / np.float32(np.log(128 / exact))
                   * np.float32(half - exact)).astype(np.int32)
    bucket = np.where(rel > 0, half, 0) + np.where(dist < exact, dist, np.minimum(far, half - 1))
    onehot = (np.arange(NBKT)[:, None] == bucket[None, :]).astype(np.float32)
    return {"constants": table, "bucket_onehot": onehot}


_INS = {"x": "x", "ctx_1024": "ctx", "mask_BxSxS2_if1": "mask", "L0_xattn_Wq": "Wq", "L0_xattn_bq": "bq",
        "L0_xattn_Wk": "Wk", "L0_xattn_bk": "bk", "L0_xattn_Wv": "Wv", "L0_xattn_bv": "bv", "L0_xattn_Wo": "Wo",
        "L0_xattn_bo": "bo", "L0_attn_Wq": "aWq", "L0_attn_Wk": "aWk", "L0_attn_Wv": "aWv", "L0_attn_Wo": "aWo",
        "L0_attn_rel_bias": "rel_bias", "L0_ffn_router_w": "router_w", "L0_ffn_router_b": "router_b",
        "L0_ffn_w1": "w1", "L0_ffn_b1": "b1", "L0_ffn_w2": "w2", "L0_ffn_b2": "b2"}


def kernel(**inputs):
    import numpy as _np
    import concourse.bacc as _bacc
    from concourse.bass_utils import run_bass_kernel_spmd as _run

    nc = _bacc.Bacc("TRN2", target_bir_lowering=False, num_devices=1)
    arrays, io = {}, {}
    for name, short in _INS.items():
        arrays[f"in_{name}"] = a = _np.ascontiguousarray(inputs[name])
        io[short] = nc.dram_tensor(f"in_{name}", a.shape, mybir.dt.from_np(a.dtype), kind="ExternalInput").ap()
    for name, a in shape_constants().items():
        arrays[f"shape_{name}"] = a
        io[name] = nc.dram_tensor(f"shape_{name}", a.shape, mybir.dt.from_np(a.dtype), kind="ExternalInput").ap()
    io["out"] = nc.dram_tensor("out", (B, SQ, D), F32, kind="ExternalOutput").ap()
    perceiver_program(nc, io)
    r = _run(nc, [arrays], core_ids=[0])
    return r.results[0]["out"]
```

```python
from contextlib import ExitStack

import concourse.bass as bass
from concourse import mybir

F32 = mybir.dt.float32
F32R = mybir.dt.float32r
BF16 = mybir.dt.bfloat16
I32 = mybir.dt.int32
U32 = mybir.dt.uint32
ALU = mybir.AluOpType
ACT = mybir.ActivationFunctionType
AX = mybir.AxisListType

P = 128
B, SQ, D, SK = 16, 64, 128, 1601
NH, DK = 16, 8
NG = 4
KS = 96
NT = -(-SK // P)
TAIL = SK - (NT - 1) * P
SKP = SK + SK % 2
CH = 4
CW = [512, 512, 512, TAIL]
NJ = 8
UNITS = CH * NJ
TOK = B * SQ
NTT = TOK // P
EPS = 1e-5
MASKED = -10000.0
MARK = -125.0 * 2.0 ** 60
MARK_TO_MASKED = 80.0 * 2.0 ** -60
CHUNK_STEPS = {0: (1, 3, 0), 1: (1, 3, 1), 2: (1, 3, 2), 3: (2, 0, 0), 4: (2, 0, 1), 5: (2, 0, 2),
               6: (2, 1, 0), 7: (2, 1, 1), 8: (2, 1, 2), 10: (2, 2, 0), 11: (2, 2, 1), 12: (2, 2, 2)}
UNIT_SLOTS = [1, 2, 3, 4, 3, 3, 4, 4, 4, 4, 0, 0, 0]
UNIT_AT = [sum(UNIT_SLOTS[:t]) for t in range(NT)]
MAX_SLOT = 10
FIRST_UNITS = [1, 0, 7, 8, 4, 12]
MARK_SLOT = 3
RELOC = 2 * 6 * 16


def tile_rows(t):
    return P if t < NT - 1 else TAIL


def cross_attention(nc, io, keep):
    ou, xall, cst, ones = keep.ou, keep.x, keep.constants, keep.ones
    ctxb, ctail, mraw = keep.context, keep.tail, keep.mask_raw
    with ExitStack() as ctx:
        def sb(name, shape, dt=F32):
            return ctx.enter_context(nc.sbuf_tensor(name, shape, dt))

        def sem(name):
            return ctx.enter_context(nc.semaphore(name))

        kst = [sb(f"key_stack{i}", [KS + 2, NG, SKP], F32R) for i in range(2)]
        vx = sb("values", [P, 2, NT, 2 * P])
        st_hi = sb("keys_hi", [P, SK], F32R)
        st_lo = sb("keys_lo", [P, SK], F32R)
        ctxT = sb("context_T", [P, 2, 512])
        probs = sb("probs", [P, 2, 1024])
        q1 = [sb(f"q_pass1_{i}", [KS, 1024], F32R) for i in range(2)]
        q2 = [sb(f"q_pass2_{i}", [KS + 2, 1024], F32R) for i in range(2)]
        qr = sb("q_roles", [P, NG, TOK])
        a1 = [sb(f"mark_pass1_{i}", [P, SK], BF16) for i in range(2)]
        a2 = [sb(f"mark_pass2_{i}", [SQ, SK], BF16) for i in range(2)]
        sjunk = sb("masked_scores_junk", [P, 2, 512], BF16)
        mx = sb("chunk_max", [P, 2, NJ, CH])
        mxr = sb("row_max", [P, NJ])
        asum = sb("mark_sum", [P, 2])
        flr = sb("max_floor", [P, 2])
        negm = sb("neg_max", [P, NJ])
        mh = sb("neg_max_hi_lo", [P, 2 * NJ])
        mrow = sb("neg_max_rows", [2 * NJ, 2, P])
        flag = sb("any_masked", [1, 2], I32)
        xn = sb("x_normed", [P, NTT, D])
        ajunk = xn[:, :, :].rearrange("p t d -> p (t d)").bitcast(BF16)[:, 0:SK]
        xnT = sb("x_normed_T", [P, TOK])
        bst = sb("ln_stats", [P, NTT, 6])
        bag = sb("ln_mean_var", [P, NTT, 2])
        rstd = sb("ln_rstd", [P, NTT])
        ident = cst[:, 0:P]
        bd = cst[0:KS, P:P + NG]
        eps = cst[:, P + NG:P + NG + 1]
        wq = sb("w_q", [P, P])
        wqr = sb("w_q_roles", [P, NG, 3, 32])
        wk = sb("w_k", [P, P])
        wv = sb("w_v", [P, P])
        bqr = sb("b_q_roles", [KS, NG])
        bk = sb("b_k", [P, 1])
        mrhs = sb("mark_rhs", [SQ, 3, 8, SQ], BF16)
        warm = sb("warm", [P, 2])

        s2 = [ctx.enter_context(nc.psum_tensor(f"scores{i}", [P, 1024], F32)) for i in range(2)]
        s1 = [ctx.enter_context(nc.psum_tensor(f"scores_rows{i}", [P, 512], F32)) for i in range(2)]
        po = ctx.enter_context(nc.psum_tensor("out_acc", [P, 512], F32))
        pc = ctx.enter_context(nc.psum_tensor("chunk", [P, 512], F32))

        const_landed = sem("const_landed")
        x_landed = sem("x_landed")
        w_landed = sem("w_landed")
        kvw_landed = sem("kvw_landed")
        ctx_landed = [sem(f"ctx_landed{i}") for i in range(2)]
        mask_landed = sem("mask_landed")
        mark_ready = sem("mark_ready")
        mark2_ready = sem("mark2_ready")
        q1_ready = sem("q1_ready")
        q2_ready = sem("q2_ready")
        reloc_landed = [sem(f"reloc_landed{i}") for i in range(2)]
        negmax_landed = sem("negmax_landed")
        tp_ready = sem("tp_ready")
        ctxT_copied = sem("ctxT_copied")
        kproj_ready = sem("kproj_ready")
        khi_ready = sem("khi_ready")
        klo_ready = sem("klo_ready")
        vproj_ready = sem("vproj_ready")
        v_copied = sem("v_copied")
        unit_ready = sem("unit_ready")
        unit_done = sem("unit_done")
        marksum_ready = sem("marksum_ready")
        max_chain = sem("max_chain")
        negmax_ready = sem("negmax_ready")
        negmax_rows = sem("negmax_rows")
        negmax_copied = sem("negmax_copied")
        scores_ready = sem("scores_ready")
        exp_done = sem("exp_done")
        pv_done = sem("pv_done")
        out_bank_free = sem("out_bank_free")
        init_done = sem("init_done")
        ones_ready = sem("ones_ready")
        dve_seq = sem("dve_seq")
        var_ready = sem("var_ready")
        std_ready = sem("std_ready")
        xn_ready = sem("xn_ready")
        xnT_ready = sem("xnT_ready")
        xnT_copied = sem("xnT_copied")
        qp_ready = sem("qp_ready")
        qr_ready = sem("qr_ready")
        qhi_ready = sem("qhi_ready")
        bq_scaled = sem("bq_scaled")
        pool_passed = sem("pool_passed")
        pe_passed = sem("pe_passed")
        dve_passed = sem("dve_passed")

        block = ctx.enter_context(nc.Block())

        FIRST_BANKS = s1 + [s2[k // 2][:, 512 * (k % 2):512 * (k % 2) + 512] for k in range(4)]

        def one(ap, b):
            return ap[b] if isinstance(b, int) else ap[bass.ds(b, 1)].squeeze(0)

        @block.sync
        def _(sp):
            sp.dma_start(xall[:, :, :], io["x"].rearrange("b s d -> (b s) d").rearrange("(t p) d -> p t d", p=P)).then_inc(x_landed, 16)
            sp.dma_start(cst[:, :], io["constants"]).then_inc(const_landed, 16)

            def load_ctx(b, par):
                src = one(io["ctx"], b)
                if not (isinstance(b, int) and b < 2):
                    sp.wait_ge(tp_ready, CH * (b - 1))
                sp.dma_start(ctxb[:, par, :, :, :].rearrange("p c j d -> p c (j d)"),
                             src[0:3 * 512, :].rearrange("(c p j) d -> p c (j d)", p=P, j=4)).then_inc(ctx_landed[par], 16)
                sp.dma_start(ctail[:, par, :], src[3 * 512:SK, :]).then_inc(ctx_landed[par], 16)

            def load_mask(b):
                if not (isinstance(b, int) and b < 1):
                    sp.wait_ge(mark_ready, b)
                for r in range(2):
                    sp.dma_start(mraw[SQ * r:SQ * r + SQ, :], one(io["mask"], b)).then_inc(mask_landed, 16)

            def relocate(b, par, half, roles=(0, 1, 2)):
                sp.wait_ge(klo_ready, CH * b + 2 * (half + 1))
                lo, hi = (0, 1024) if half == 0 else (1024, SK)
                if half == 0 and not (isinstance(b, int) and b < 2):
                    sp.wait_ge(scores_ready, NT * (b - 2) + 8)
                for role in roles:
                    src = (st_hi, st_lo, st_hi)[role]
                    for g in range(NG):
                        sp.dma_start(kst[par][32 * role:32 * role + 32, g, lo:hi].bitcast(F32),
                                     src[32 * g:32 * g + 32, lo:hi].bitcast(F32)).then_inc(reloc_landed[half], 16)

            def send_negmax(b, par):
                sp.wait_ge(negmax_copied, b + 1)
                sp.wait_ge(q2_ready, b + 1)
                for r in range(2):
                    sp.dma_start(q2[par][KS + r:KS + r + 1, :].rearrange("p (k c) -> p k c", c=P).bitcast(F32),
                                 mrow[NJ * r:NJ * r + NJ, par, :]).then_inc(negmax_landed, 16)

            load_ctx(0, 0)
            sp.dma_start(wk[:, :], io["Wk"]).then_inc(kvw_landed, 16)
            sp.dma_start(wv[:, :], io["Wv"]).then_inc(kvw_landed, 16)
            sp.dma_start(bk[:, :], io["bk"].rearrange("(p a) -> p a", a=1)).then_inc(kvw_landed, 16)
            sp.dma_start(wq[:, :], io["Wq"]).then_inc(w_landed, 16)
            with nc.allow_non_contiguous_dma(reason="a bias of 128 values"):
                for r in range(3):
                    sp.dma_start(bqr[32 * r:32 * r + 32, :], io["bq"].rearrange("(g c) -> c g", c=32)).then_inc(w_landed, 16)
            load_mask(0)
            load_ctx(1, 1)
            relocate(0, 0, 0)
            relocate(0, 0, 1)
            load_mask(1)
            relocate(1, 1, 0, (0, 1))
            send_negmax(0, 0)
            relocate(1, 1, 0, (2,))

            def batch(b, par, chunks, pass1):
                if chunks:
                    load_ctx(b + 2, par)
                    load_mask(b + 2)
                if pass1:
                    relocate(b + 1, 1 - par, 1)
                if chunks:
                    relocate(b + 2, par, 0, (0, 1))
                if pass1:
                    send_negmax(b + 1, 1 - par)
                if chunks:
                    relocate(b + 2, par, 0, (2,))

            with sp.Fori(0, B // 2 - 1) as i:
                batch(2 * i, 0, True, True)
                batch(2 * i + 1, 1, True, True)
            batch(B - 2, 0, False, True)
            sp.wait_ge(tp_ready, CH * B)
            keep.weights.load(sp, io)
            sp.wait_ge(mark_ready, B)
            keep.weights.load_rest(sp, io)

        @block.gpsimd
        def _(pool):
            pool.memset(vx[:, 1, :, :], 0.0).then_inc(ones_ready, 1)
            pool.wait_ge(ones_ready, 1)
            pool.memset(vx[:, 1, :, :].rearrange("p t (h e) -> p (t h) e", e=16)[:, :, DK:DK + 1], 1.0).then_inc(init_done, 1)
            for k in range(2):
                pool.memset(kst[k][0:KS, :, SK:SKP].bitcast(F32), 0.0).then_inc(ones_ready, 1)
            pool.wait_ge(ones_ready, 3)

            def ones_rows(k):
                pool.memset(kst[k][KS:KS + 2, :, :].bitcast(F32), 1.0).then_inc(ones_ready, 1)
                pool.wait_ge(ones_ready, 4 + k)

            def spread(dst, b, ready):
                out = dst[0:KS, :].rearrange("p (g h q) -> p g h q", g=NG, h=4)
                for h in range(4):
                    op = pool.tensor_tensor(out[:, :, h, :], qr[0:KS, :, b * SQ:(b + 1) * SQ] if isinstance(b, int)
                                            else qr[0:KS, :, bass.ds(b * SQ, SQ)],
                                            bd[:, h:h + 1].unsqueeze(1).to_broadcast([KS, NG, SQ]), ALU.mult)
                op.then_inc(ready, 1)

            def marks(b, par):
                if not (isinstance(b, int) and b < 2):
                    pool.wait_ge(unit_done, UNITS * (b - 1))
                pool.wait_ge(mask_landed, 32 * (b + 1))
                pool.sem_inc(pool_passed, 1)
                pool.tensor_scalar(a1[par][:, :], mraw[:, :], 0, MARK, ALU.is_le, ALU.mult).then_inc(mark_ready, 1)

            def marks2(b, par):
                pool.wait_ge(mark_ready, b + 1)
                pool.sem_inc(pool_passed, 1)
                pool.tensor_copy(a2[par][:, :], a1[par][0:SQ, :]).then_inc(mark2_ready, 1)

            ones_rows(0)
            marks(0, 0)
            pool.wait_ge(mark_ready, 1)
            ones_rows(1)
            marks2(0, 0)
            pool.wait_ge(mark2_ready, 1)
            pool.wait_ge(const_landed, 16)
            pool.wait_ge(qr_ready, NG)
            spread(q1[0], 0, q1_ready)
            spread(q2[0], 0, q2_ready)
            spread(q1[1], 1, q1_ready)
            marks(1, 1)
            spread(q2[1], 1, q2_ready)
            marks2(1, 1)

            def batch(b, par):
                pool.wait_ge(unit_ready, UNITS * (b + 1))
                pool.sem_inc(pool_passed, 1)
                spread(q1[par], b + 2, q1_ready)
                marks(b + 2, par)
                pool.wait_ge(scores_ready, NT * (b + 1))
                pool.sem_inc(pool_passed, 1)
                spread(q2[par], b + 2, q2_ready)
                marks2(b + 2, par)

            with pool.Fori(0, B // 2 - 1) as i:
                batch(2 * i, 0)
                batch(2 * i + 1, 1)

        @block.scalar
        def _(act):
            act.wait_ge(const_landed, 16)
            act.wait_ge(var_ready, 1)
            nc.scalar.activation(rstd[:, :], bag[:, :, 1], ACT.Sqrt, bias=eps).then_inc(std_ready, 1)
            for k in range(2):
                nc.scalar.activation(warm[:, k:k + 1], eps, ACT.Exp).then_inc(exp_done, 1)

            def chunk_copy(b, par, c, step, pc=pc):
                q = CH * b + c
                w = CW[c]
                if step == 0:
                    act.wait_ge(tp_ready, q + 1)
                    if c < 3:
                        nc.scalar.activation(ctxT[:, c % 2, :].rearrange("d (p j) -> d j p", j=4),
                                             pc[:, :].rearrange("d (j p) -> d j p", j=4), ACT.Copy).then_inc(ctxT_copied, 1)
                    else:
                        nc.scalar.activation(ctxT[:, c % 2, 0:w], pc[:, 0:w], ACT.Copy).then_inc(ctxT_copied, 1)
                elif step == 1:
                    act.wait_ge(kproj_ready, q + 1)
                    if not (isinstance(b, int) and b < 1):
                        act.wait_ge(reloc_landed[c // 2], RELOC * b)
                    nc.scalar.activation(st_hi[:, 512 * c:512 * c + w], pc[:, 0:w], ACT.Identity, bias=bk[:, 0:1]).then_inc(khi_ready, 1)
                else:
                    act.wait_ge(vproj_ready, q + 1)
                    if not (isinstance(b, int) and b < 2):
                        act.wait_ge(pv_done, NT * (b - 2) + min(4 * c + 3, NT - 1) + 3)
                    n = 4 if c < 3 else 1
                    r = P if c < 3 else TAIL
                    nc.scalar.activation(vx[0:r, par, 4 * c:4 * c + n, :].rearrange("p t (h e) -> p t h e", e=16)[:, :, :, 0:DK],
                                         pc[0:r, 0:n * P].rearrange("p (t h d) -> p t h d", t=n, d=DK), ACT.Copy).then_inc(v_copied, 1)

            def exp(b, par, t):
                s = NT * b + t
                k = (NT * par + t) % 2
                r = tile_rows(t)
                act.wait_ge(scores_ready, s + 1)
                act.wait_ge(pv_done, s + 1)
                nc.scalar.activation(probs[0:r, k, :], s2[k][0:r, :], ACT.Exp).then_inc(exp_done, 1)

            def mark_sum(b, par):
                act.wait_ge(mark_ready, b + 1)
                nc.scalar.activation(ajunk[:, :], a1[par][:, :], ACT.Identity, accum_out=asum[:, par:par + 1]).then_inc(marksum_ready, 1)

            def query_hi(g):
                act.wait_ge(qp_ready, g + 1)
                nc.scalar.activation(qr[0:KS, g, :].bitcast(F32R), s2[(g + 1) % 2][0:KS, :], ACT.Identity,
                                     bias=bqr[:, g:g + 1]).then_inc(qhi_ready, 1)

            act.wait_ge(kvw_landed, 48)
            act.wait_ge(bq_scaled, 1)
            act.wait_ge(init_done, 1)
            for c in (0, 2):
                for k in (c, c + 1):
                    chunk_copy(0, 0, k, 0, (pc, po)[k % 2])
                if c == 2:
                    query_hi(0)
                    query_hi(1)
                for k in (c, c + 1):
                    chunk_copy(0, 0, k, 1, (pc, po)[k % 2])
                if c == 2:
                    query_hi(2)
                    query_hi(3)
                for k in (c, c + 1):
                    chunk_copy(0, 0, k, 2, (pc, po)[k % 2])
            act.wait_ge(xnT_ready, 1)
            mark_sum(0, 0)
            act.wait_ge(init_done, 2)
            for c in range(3):
                for step in range(3):
                    chunk_copy(1, 1, c, step)

            def batch(b, par, chunks, pass1):
                for t in range(NT):
                    ahead, c, step = CHUNK_STEPS.get(t - 1, (9, 0, 0))
                    if (ahead == 1 and pass1) or (ahead == 2 and chunks):
                        chunk_copy(b + ahead, (par + ahead) % 2, c, step)
                    exp(b, par, t)
                    if t == MARK_SLOT and pass1:
                        mark_sum(b + 1, 1 - par)
                if chunks:
                    ahead, c, step = CHUNK_STEPS[NT - 1]
                    chunk_copy(b + ahead, par, c, step)

            with act.Fori(0, B // 2 - 1) as i:
                batch(2 * i, 0, True, True)
                batch(2 * i + 1, 1, True, True)
            batch(B - 2, 0, False, True)
            batch(B - 1, 1, False, False)

        @block.tensor
        def _(pe):
            def turn_tokens():
                for n in range(NTT):
                    pe.wait_ge(xn_ready, n + 1)
                    last = nc.tensor.transpose(s2[0][:, P * n:P * n + P], xn[:, n, :], ident)
                last.then_inc(xnT_ready, 1)

            def query(g):
                pe.wait_ge(xnT_copied, 1)
                if g >= 2:
                    pe.wait_ge(qr_ready, g - 1)
                for n in range(2):
                    last = nc.tensor.matmul(s2[(g + 1) % 2][0:KS, 512 * n:512 * n + 512], wqr[:, g, :, :].rearrange("p r c -> p (r c)"),
                                            xnT[:, 512 * n:512 * n + 512], start=True, stop=True)
                last.then_inc(qp_ready, 1)

            def chunk(b, par, c, step, pc=pc):
                q = CH * b + c
                w = CW[c]
                if step == 0:
                    if c == 0:
                        pe.wait_ge(ctx_landed[par], 16 * (b - par) + 32)
                    if not isinstance(b, int) or b > 0:
                        pe.wait_ge(v_copied, q)
                    elif c >= 2:
                        pe.wait_ge(v_copied, c - 1)
                    for j in range(4 if c < 3 else 1):
                        last = (nc.tensor.transpose(pc[:, P * j:P * j + P], ctxb[:, par, c, j, :], ident) if c < 3 else
                                nc.tensor.transpose(pc[:, 0:TAIL], ctail[:, par, :], ident[0:TAIL, 0:TAIL]))
                    last.then_inc(tp_ready, 1)
                elif step == 1:
                    pe.wait_ge(ctxT_copied, q + 1)
                    nc.tensor.matmul(pc[:, 0:w], wk[:, :], ctxT[:, c % 2, 0:w], start=True, stop=True).then_inc(kproj_ready, 1)
                else:
                    pe.wait_ge(klo_ready, q + 1)
                    for j in range(4 if c < 3 else 1):
                        r = P if c < 3 else TAIL
                        last = nc.tensor.matmul(pc[0:r, P * j:P * j + P], ctxT[:, c % 2, P * j:P * j + r], wv[:, :], start=True, stop=True)
                    last.then_inc(vproj_ready, 1)

            def unit(b, par, k, banks=s1):
                c, j = divmod(k, NJ)
                u = UNITS * b + k
                if k == 0:
                    pe.wait_ge(q1_ready, b + 1)
                if k in (0, 2 * NJ):
                    pe.wait_ge(reloc_landed[c // 2], RELOC * (b + 1))
                if not (isinstance(b, int) and u < len(banks)):
                    pe.wait_ge(unit_done, u + 1 - len(banks))
                w = CW[c] + CW[c] % 2
                nc.tensor.matmul(banks[k % len(banks)][:, 0:w], q1[par][0:KS, P * j:P * j + P],
                                 kst[par][0:KS, j // 2, 512 * c:512 * c + w], start=True, stop=True).then_inc(unit_ready, 1)

            def max_rows(b, par):
                pe.wait_ge(negmax_ready, b + 1)
                nc.tensor.transpose(s1[0][0:2 * NJ, 0:P], mh[:, :], ident)
                nc.tensor.matmul(s1[0][0:1, P:P + 1], asum[:, par:par + 1], ones[:, :], start=True, stop=True).then_inc(negmax_rows, 1)

            def score_rows(par, t, p0, p1, first):
                k = (NT * par + t) % 2
                r = tile_rows(t)
                for g in range(NG):
                    last = nc.tensor.matmul(s2[k][0:r, 256 * g:256 * g + 256], kst[par][p0:p1, g, P * t:P * t + r],
                                            q2[par][p0:p1, 256 * g:256 * g + 256], start=first and g % 2 == 0, stop=True,
                                            skip_group_check=True)
                return last

            def mark_scores(par, t):
                k = (NT * par + t) % 2
                r = tile_rows(t)
                for f in range(3):
                    for n in range(2):
                        nc.tensor.matmul(s2[k][0:r, 512 * n:512 * n + 512], a2[par][:, P * t:P * t + r],
                                         mrhs[:, f, :, :].rearrange("p h q -> p (h q)"), start=False, stop=True, skip_group_check=True)

            def scores(b, par, t, masked):
                if t == 0:
                    pe.wait_ge(negmax_landed, 32 * (b + 1))
                pe.wait_ge(exp_done, NT * b + t + 1)
                with pe.If(masked > 0):
                    score_rows(par, t, 0, KS, True)
                    mark_scores(par, t)
                    score_rows(par, t, KS, KS + 2, False).then_inc(scores_ready, 1)
                with pe.Else():
                    score_rows(par, t, 0, KS + 2, True).then_inc(scores_ready, 1)

            def pv(b, par, t, half):
                s = NT * b + t
                k = (NT * par + t) % 2
                r = tile_rows(t)
                if half == 0:
                    pe.wait_ge(exp_done, s + 3)
                    if t == 0:
                        pe.wait_ge(out_bank_free, b + 1)
                for c in range(4):
                    j = 4 * half + c
                    last = nc.tensor.matmul(po[32 * c:32 * c + 32, P * half:P * half + P], vx[0:r, par, t, 32 * j:32 * j + 32],
                                            probs[0:r, k, P * j:P * j + P], start=(t == 0 and half == 0), stop=(t == NT - 1), skip_group_check=True)
                if half == 1:
                    last.then_inc(pv_done, 1)

            pe.wait_ge(const_landed, 16)
            for k in range(2):
                nc.tensor.transpose(po[:, 0:P], ident, ident).then_inc(pv_done, 1)
            pe.wait_ge(kvw_landed, 48)
            for c in (0, 2):
                for k in (c, c + 1):
                    chunk(0, 0, k, 0, (pc, po)[k % 2])
                if c == 2:
                    query(0)
                    query(1)
                for k in (c, c + 1):
                    chunk(0, 0, k, 1, (pc, po)[k % 2])
                if c == 2:
                    query(2)
                    query(3)
                for k in (c, c + 1):
                    chunk(0, 0, k, 2, (pc, po)[k % 2])
                if c == 0:
                    turn_tokens()
            pe.wait_ge(ones_ready, 3)
            for n in range(len(FIRST_UNITS)):
                chunk(1, 1, n // 3, n % 3)
                for k in range(sum(FIRST_UNITS[:n]), sum(FIRST_UNITS[:n + 1])):
                    unit(0, 0, k, FIRST_BANKS)
            pe.wait_ge(init_done, 2)
            pe.wait_ge(ones_ready, 5)
            max_rows(0, 0)
            for n in range(len(FIRST_UNITS), 9):
                chunk(1, 1, n // 3, n % 3)

            def batch(b, par, chunks, pass1):
                pe.wait_ge(negmax_copied, b + 1)
                pe.wait_ge(mark2_ready, b + 1)
                pe.sem_inc(pe_passed, 1)
                masked = pe.value_load(flag[0:1, par:par + 1], min_val=0, max_val=1)
                for t in range(NT):
                    scores(b, par, t, masked)
                    fill = list(range(UNIT_AT[t], UNIT_AT[t] + UNIT_SLOTS[t])) if pass1 else []
                    for half in range(2):
                        if fill:
                            unit(b + 1, 1 - par, fill.pop(0))
                        if t > 0:
                            pv(b, par, t - 1, half)
                    if len(fill) > 1:
                        unit(b + 1, 1 - par, fill.pop(0))
                    ahead, c, step = CHUNK_STEPS.get(t, (9, 0, 0))
                    here = t < NT - 1 and ((ahead == 1 and pass1) or (ahead == 2 and chunks))
                    if here:
                        chunk(b + ahead, (par + ahead) % 2, c, step)
                    for k in fill:
                        unit(b + 1, 1 - par, k)
                    if t == MAX_SLOT and pass1:
                        max_rows(b + 1, 1 - par)
                pv(b, par, NT - 1, 0)
                pv(b, par, NT - 1, 1)
                if chunks:
                    ahead, c, step = CHUNK_STEPS[NT - 1]
                    chunk(b + ahead, par, c, step)

            with pe.Fori(0, B // 2 - 1) as i:
                batch(2 * i, 0, True, True)
                batch(2 * i + 1, 1, True, True)
            batch(B - 2, 0, False, True)
            batch(B - 1, 1, False, False)

        @block.vector
        def _(dve):
            seq = [0]

            def link(op):
                seq[0] += 1
                op.then_inc(dve_seq, 1)
                dve.wait_ge(dve_seq, seq[0])

            link(nc.vector.memset(vx[:, 0, :, :], 0.0))
            nc.vector.memset(vx[:, 0, :, :].rearrange("p t (h e) -> p (t h) e", e=16)[:, :, DK:DK + 1], 1.0).then_inc(init_done, 1)
            nc.vector.memset(ones[:, :], 1.0)
            nc.vector.memset(sjunk[:, 0, 0:2], 0.0).then_inc(out_bank_free, 1)
            dve.wait_ge(x_landed, 16)
            for n in range(NTT):
                last = nc.vector.bn_stats(bst[:, n, :], xall[:, n, :])
            link(last)
            for n in range(NTT):
                last = nc.vector.bn_aggr(bag[:, n, :], bst[:, n, :])
            last.then_inc(var_ready, 1)
            dve.wait_ge(w_landed, 16 * 4)
            link(nc.vector.tensor_scalar(wq[:, :], wq[:, :], DK ** -0.5, None, ALU.mult))
            for r in range(3):
                nc.vector.tensor_copy(wqr[:, :, r, :], wq[:, :].rearrange("p (g c) -> p g c", c=32))
            nc.vector.tensor_scalar(bqr[:, :], bqr[:, :], DK ** -0.5, None, ALU.mult).then_inc(bq_scaled, 1)
            dve.wait_ge(bq_scaled, 1)
            dve.wait_ge(std_ready, 1)
            dve.wait_ge(var_ready, 1)
            link(nc.vector.reciprocal(rstd[:, :], rstd[:, :]))
            for n in range(NTT):
                nc.vector.tensor_scalar(xn[:, n, :], xall[:, n, :], bag[:, n, 0:1], rstd[:, n:n + 1],
                                        ALU.subtract, ALU.mult).then_inc(xn_ready, 1)
            dve.wait_ge(const_landed, 16)
            for f, w in enumerate((1.0, -1.0, MARK_TO_MASKED)):
                nc.vector.tensor_scalar(mrhs[:, f, :, :], ident[0:SQ, 0:SQ].unsqueeze(1).to_broadcast([SQ, 8, SQ]), w, None, ALU.mult)

            def query_lo(g):
                dve.wait_ge(qhi_ready, g + 1)
                nc.vector.scalar_tensor_tensor(out=qr[64:96, g, :], in0=s2[(g + 1) % 2][64:96, :], scalar=bqr[64:96, g:g + 1],
                                               in1=qr[64:96, g, :], op0=ALU.add, op1=ALU.subtract).then_inc(qr_ready, 1)

            def key_lo(b, c, pc=pc):
                q = CH * b + c
                w = CW[c]
                dve.wait_ge(khi_ready, q + 1)
                nc.vector.scalar_tensor_tensor(out=st_lo[:, 512 * c:512 * c + w], in0=pc[:, 0:w], scalar=bk[:, 0:1],
                                               in1=st_hi[:, 512 * c:512 * c + w].bitcast(F32), op0=ALU.add,
                                               op1=ALU.subtract).then_inc(klo_ready, 1)

            def unit(b, par, k, banks=s1):
                c, j = divmod(k, NJ)
                if k == 0:
                    dve.wait_ge(mark_ready, b + 1)
                dve.wait_ge(unit_ready, UNITS * b + k + 1)
                dve.sem_inc(dve_passed, 1)
                if banks is not s1 and k >= 2:
                    dve.wait_ge(unit_done, k - 1)
                nc.vector.tensor_tensor_reduce(out=sjunk[:, k % 2, 0:CW[c]], in0=banks[k % len(banks)][:, 0:CW[c]], in1=a1[par][:, 512 * c:512 * c + CW[c]],
                                               scale=1.0, scalar=-3.0e38, op0=ALU.add, op1=ALU.max,
                                               accum_out=mx[:, par, j, c:c + 1]).then_inc(unit_done, 1)

            def find_max(b, par):
                n = 5 * b

                def then(op, k):
                    op.then_inc(max_chain, 1)
                    dve.wait_ge(max_chain, n + k)

                dve.wait_ge(marksum_ready, b + 1)
                nc.vector.tensor_scalar(flr[:, 0:1], asum[:, par:par + 1], 0.0, -3.0e38, ALU.is_equal, ALU.mult).then_inc(max_chain, 1)
                dve.wait_ge(unit_done, UNITS * (b + 1))
                nc.vector.tensor_reduce(mxr[:, :], mx[:, par, :, :], axis=AX.X, op=ALU.max).then_inc(max_chain, 1)
                dve.wait_ge(max_chain, n + 2)
                then(nc.vector.tensor_scalar(flr[:, 1:2], flr[:, 0:1], MASKED, None, ALU.add), 3)
                then(nc.vector.tensor_scalar(negm[:, :], mxr[:, :], flr[:, 1:2], -1.0, ALU.max, ALU.mult), 4)
                then(nc.vector.tensor_copy(mh[:, 0:NJ].bitcast(F32R), negm[:, :]), 5)
                nc.vector.tensor_tensor(mh[:, NJ:2 * NJ].bitcast(F32R), negm[:, :], mh[:, 0:NJ], ALU.subtract).then_inc(negmax_ready, 1)

            def copy_max(b, par):
                dve.wait_ge(negmax_rows, b + 1)
                nc.vector.tensor_copy(mrow[:, par, :], s1[0][0:2 * NJ, 0:P])
                nc.vector.tensor_scalar(flag[0:1, par:par + 1], s1[0][0:1, P:P + 1], 0.0, None, ALU.is_lt).then_inc(negmax_copied, 1)

            key_lo(0, 0, pc)
            key_lo(0, 1, po)
            dve.wait_ge(xnT_ready, 1)
            nc.vector.tensor_copy(xnT[:, :], s2[0][:, :]).then_inc(xnT_copied, 1)
            query_lo(0)
            query_lo(1)
            key_lo(0, 2, pc)
            key_lo(0, 3, po)
            query_lo(2)
            query_lo(3)
            for n in range(len(FIRST_UNITS)):
                if n % 3 == 2:
                    key_lo(1, n // 3)
                for k in range(sum(FIRST_UNITS[:n]), sum(FIRST_UNITS[:n + 1])):
                    unit(0, 0, k, FIRST_BANKS)
            find_max(0, 0)
            copy_max(0, 0)
            key_lo(1, 2)

            def batch(pair, par, chunks, pass1):
                b = 2 * pair + par
                for t in range(NT):
                    fill = list(range(UNIT_AT[t], UNIT_AT[t] + UNIT_SLOTS[t])) if pass1 else []
                    ahead, c, step = CHUNK_STEPS.get(t - 1, (9, 0, 0))
                    if step == 1 and ((ahead == 1 and pass1) or (ahead == 2 and chunks)):
                        key_lo(b + ahead, c)
                    for k in fill:
                        unit(b + 1, 1 - par, k)
                    if t == MAX_SLOT - 1 and pass1:
                        find_max(b + 1, 1 - par)
                    if t == MAX_SLOT + 1 and pass1:
                        copy_max(b + 1, 1 - par)
                dve.wait_ge(pv_done, NT * (b + 1) + 2)
                nc.vector.tensor_copy(ou[:, pair, :, par, :] if isinstance(b, int) else ou[:, bass.ds(pair, 1), :, par, :].squeeze(1),
                                      po[:, 0:2 * P].rearrange("p (k q) -> p k q", q=SQ)).then_inc(out_bank_free, 1)

            with dve.Fori(0, B // 2 - 1) as i:
                batch(i, 0, True, True)
                batch(i, 1, True, True)
            batch(B // 2 - 1, 0, False, True)
            batch(B // 2 - 1, 1, False, False)


KVH, DH = 4, 64
GA = 4
NE, NHID = 8, 512
HC = NHID // P
NBKT = 32
FAR = -1.0e30


def self_attention(nc, io, keep):
    ou, x, cst, weights = keep.ou, keep.x, keep.constants, keep.weights
    ident = cst[:, 0:P]
    eps = cst[:, P + NG:P + NG + 1]
    with ExitStack() as ctx:
        def sb(name, shape, dt=F32):
            return ctx.enter_context(nc.sbuf_tensor(name, shape, dt))

        def sem(name):
            return ctx.enter_context(nc.semaphore(name))

        pair_sum = sb("w_pair_sums", [P, 2, 3, 2 * P])
        pair_sum_o = sb("w_pair_sums_out", [P, 2, 2 * P])
        wsum = sb("w_group_sums", [P, 4, 2 * P])
        wT = sb("w_attn_T", [P, 4, 2 * P])
        rbm = sb("rel_bias_mean", [NBKT, KVH])
        rel = sb("rel_position_bias", [KVH, 2 * SQ])
        bias_rev = sb("score_bias_reversed", [SQ, KVH, SQ])
        bias = sb("score_bias", [P, KVH, P])
        rd = sb("out_rdenom", [P, 2, 2, 2, 2, 4])
        on = sb("out_norm", [P, NTT, P])
        oT = sb("out_T", [P, 2, 2, P])
        bst = sb("ln_stats_b", [P, NTT, 6])
        bag = sb("ln_aggr_b", [P, NTT, 2])
        rstd = sb("ln_rstd_b", [P, NTT])
        xn = sb("x_normed_b", [P, NTT, D])
        xnT = sb("x_normed_T_b", [P, TOK])
        qT = sb("attn_q_T", [P, KVH, TOK])
        kT = sb("attn_k_T", [P, 2, TOK])
        va = sb("attn_v", [P, NTT, 2 * P])
        sc = sb("attn_scores", [P, NTT, KVH, P])
        ngm = sb("attn_negmax", [P, NTT, KVH])
        pr = sb("attn_exp", [P, NTT, KVH, P])
        pn = sb("attn_probs", [P, 2, KVH, P])
        den = sb("attn_denom", [P, NTT, KVH])
        rden = sb("attn_rdenom", [P, NTT, KVH])
        prT = sb("attn_probs_T", [P, 2, KVH * P])
        aoT = sb("attn_out_T", [P, 2, 2 * P])
        wide = [ctx.enter_context(nc.psum_tensor(f"bank_pair{i}", [P, 1024], F32)) for i in range(2)]
        ps = [None] * 4 + [ctx.enter_context(nc.psum_tensor(f"bank{i}", [P, 512], F32)) for i in range(4, 8)]

        def half_bank(k):
            return wide[k // 2][:, 512 * (k % 2):512 * (k % 2) + 512]

        dve_seq = sem("attn_dve_seq")
        pool_seq = sem("attn_pool_seq")
        rbm_ready = sem("rbm_ready")
        rel_ready = sem("rel_ready")
        rel_copied = sem("rel_copied")
        rev_landed = sem("rev_landed")
        bo_added = sem("bo_added")
        far_set = sem("far_set")
        zeros_set = sem("zeros_set")
        sums_ready = sem("group_sums_ready")
        wT_ready = sem("wT_ready")
        wT_copied = sem("wT_copied")
        bias_ready = sem("bias_ready")
        o_turned = sem("o_turned")
        o_normed = sem("o_normed")
        oT_ready = sem("oT_ready")
        oT_copied = sem("oT_copied")
        y1_ready = sem("y1_ready")
        x1_ready = sem("x1_ready")
        var_ready = sem("attn_var_ready")
        std_ready = sem("attn_std_ready")
        xn_ready = sem("attn_xn_ready")
        xnT_ready = sem("attn_xnT_ready")
        xnT_copied = sem("attn_xnT_copied")
        proj_ready = sem("attn_proj_ready")
        proj_copied = sem("attn_proj_copied")
        v_ready = sem("attn_v_ready")
        v_copied = sem("attn_v_copied")
        s_ready = sem("attn_s_ready")
        s_biased = sem("attn_s_biased")
        max_ready = sem("attn_max_ready")
        e_ready = sem("attn_e_ready")
        rden_ready = sem("attn_rden_ready")
        p_ready = sem("attn_p_ready")
        pT_ready = sem("attn_pT_ready")
        pT_copied = sem("attn_pT_copied")
        ao_ready = sem("attn_ao_ready")
        ao_copied = sem("attn_ao_copied")
        y2_ready = sem("y2_ready")
        block = ctx.enter_context(nc.Block())

        @block.sync
        def _(sp):
            keep.expert_weights.load_first(sp, io)
            sp.wait_ge(rel_copied, 1)
            for h in range(KVH):
                row = rel[h:h + 1, :]
                sp.dma_start(bias_rev[:, h, :], bass.AP(row.tensor, row.offset, [row.ap[0], [1, SQ], [1, SQ]])).then_inc(rev_landed, 16)

        @block.gpsimd
        def _(pool):
            pool.wait_ge(weights.landed, 16 * weights.count)
            pool.tensor_tensor(x[:, :, :], x[:, :, :], weights.bo.unsqueeze(1).to_broadcast([P, NTT, P]), ALU.add).then_inc(bo_added, 1)
            for k in range(2):
                pool.tensor_tensor(pair_sum[:, k, :, :], weights.qkv[:, :, 2 * k, :], weights.qkv[:, :, 2 * k + 1, :], ALU.add)
                op = pool.tensor_tensor(pair_sum_o[:, k, :], weights.o[:, 2 * k, :], weights.o[:, 2 * k + 1, :], ALU.add)
            op.then_inc(pool_seq, 1)
            pool.wait_ge(pool_seq, 1)
            pool.tensor_tensor(wsum[:, 0:3, :], pair_sum[:, 0, :, :], pair_sum[:, 1, :, :], ALU.add)
            pool.tensor_tensor(wsum[:, 3, :], pair_sum_o[:, 0, :], pair_sum_o[:, 1, :], ALU.add).then_inc(sums_ready, 1)
            pool.wait_ge(sums_ready, 1)
            for h in range(KVH):
                r = DH * (1 - h % 2)
                pool.memset(qT[r:r + DH, h, :], 0.0).then_inc(zeros_set, 1)
                pool.wait_ge(zeros_set, h + 1)
            for n in range(NTT):
                pool.wait_ge(rden_ready, n + 1)
                if n >= 2:
                    pool.wait_ge(pT_ready, n - 1)
                pool.tensor_tensor(pn[:, n % 2, :, :], pr[:, n, :, :], rden[:, n, :].unsqueeze(2).to_broadcast([P, KVH, P]), ALU.mult).then_inc(p_ready, 1)

        @block.scalar
        def _(act):
            for m in range(NTT // 2):
                act.wait_ge(oT_ready, m + 1)
                nc.scalar.activation(oT[:, m % 2, :, :].rearrange("p n t -> p (n t)"), ps[4 + m % 2][:, 0:2 * P], ACT.Copy).then_inc(oT_copied, 1)
                if m % 2 == 1:
                    act.wait_ge(var_ready, m // 2 + 1)
                    h = 4 * (m // 2)
                    nc.scalar.activation(rstd[:, h:h + 4], bag[:, h:h + 4, 1], ACT.Sqrt, bias=eps).then_inc(std_ready, 1)
                if m == 2:
                    act.wait_ge(wT_ready, 1)
                    for k in range(4):
                        op = nc.scalar.activation(wT[:, k, :], (wide[0][:, 0:256], wide[0][:, 256:512], wide[0][:, 512:768], wide[0][:, 768:1024])[k],
                                                  ACT.Copy, scale=0.25 if k in (1, 2) else 1.0)
                    op.then_inc(wT_copied, 1)
            for th in range(2):
                for k in range(4):
                    act.wait_ge(proj_ready, 4 * th + k + 1)
                    if k < 2:
                        for r in range(2):
                            op = nc.scalar.activation(qT[DH * r:DH * r + DH, 2 * k + r, 512 * th:512 * th + 512], ps[4 + k][DH * r:DH * r + DH, :], ACT.Copy)
                    else:
                        op = nc.scalar.activation(kT[:, k % 2, 512 * th:512 * th + 512], ps[4 + k][:, :], ACT.Copy)
                    op.then_inc(proj_copied, 1)
            for n in range(NTT + 2):
                if n < NTT:
                    act.wait_ge(max_ready, n + 1)
                    for h in range(KVH):
                        op = nc.scalar.activation(pr[:, n, h, :], sc[:, n, h, :], ACT.Exp, bias=ngm[:, n, h:h + 1],
                                                  accum_out=den[:, n, h:h + 1])
                    op.then_inc(e_ready, 1)
                if n >= 2:
                    act.wait_ge(pT_ready, n - 1)
                    nc.scalar.activation(prT[:, n % 2, :], half_bank(n % 2), ACT.Copy).then_inc(pT_copied, 1)
            act.wait_ge(keep.var_ready, 1)
            nc.scalar.activation(keep.rstd[:, 0:NTT // 2], keep.mean_var[:, 0:NTT // 2, 1], ACT.Sqrt, bias=eps).then_inc(keep.std_ready, 1)

        @block.tensor
        def _(pe):
            pe.wait_ge(rbm_ready, 1)
            nc.tensor.matmul(ps[7][0:KVH, 0:2 * SQ - 1], rbm[:, :], weights.onehot, start=True, stop=True).then_inc(rel_ready, 1)

            def turn(m):
                if m >= 2:
                    pe.wait_ge(o_normed, m - 1)
                for n in range(2):
                    for k in range(4):
                        last = nc.tensor.transpose(wide[m % 2][:, 512 * n + P * k:512 * n + P * k + P],
                                                   ou[:, 2 * m + n, k, :, :].rearrange("p b q -> p (b q)"), ident)
                last.then_inc(o_turned, 1)

            def turn_back(m):
                pe.wait_ge(o_normed, m + 1)
                if m >= 2:
                    pe.wait_ge(oT_copied, m - 1)
                for n in range(2):
                    last = nc.tensor.transpose(ps[4 + m % 2][:, P * n:P * n + P], on[:, 2 * m + n, :], ident)
                last.then_inc(oT_ready, 1)

            def project(m):
                pe.wait_ge(oT_copied, m + 1)
                if m == 0:
                    pe.wait_ge(weights.landed, 16 * weights.count)
                if m == 1:
                    pe.wait_ge(rel_copied, 1)
                if m >= 2:
                    pe.wait_ge(x1_ready, m - 1)
                for n in range(2):
                    last = nc.tensor.matmul(ps[6 + m % 2][:, P * n:P * n + P], oT[:, m % 2, n, :], weights.out1, start=True, stop=True)
                last.then_inc(y1_ready, 1)

            def turn_tokens(hf):
                for n in range(4):
                    pe.wait_ge(xn_ready, 4 * hf + n + 1)
                    last = nc.tensor.transpose(half_bank(2 + hf)[:, P * n:P * n + P], xn[:, 4 * hf + n, :], ident)
                last.then_inc(xnT_ready, 1)

            turn(0)
            turn(1)
            turn_back(0)
            turn(2)
            project(0)
            turn_back(1)
            turn(3)
            project(1)
            turn_back(2)
            pe.wait_ge(sums_ready, 1)
            pe.wait_ge(o_normed, 3)
            for k in range(4):
                for h in range(2):
                    last = nc.tensor.transpose(wide[0][:, 256 * k + P * h:256 * k + P * h + P], wsum[:, k, P * h:P * h + P], ident)
            last.then_inc(wT_ready, 1)
            project(2)
            turn_back(3)
            turn_tokens(0)
            project(3)
            pe.wait_ge(rev_landed, 16 * KVH)
            pe.wait_ge(oT_copied, NTT // 2)
            nc.tensor.matmul(ps[5][:, 0:KVH * SQ], weights.flip, bias_rev[:, :, :].rearrange("p h k -> p (h k)"), start=True, stop=True).then_inc(bias_ready, 1)
            pe.wait_ge(wT_copied, 1)

            def project_tokens(th):
                pe.wait_ge(xnT_copied, th + 1)
                for k in range(4):
                    if th == 0 and k == 1:
                        pe.wait_ge(far_set, 2)
                    if th == 0 and k == 2:
                        pe.wait_ge(x1_ready, NTT // 2)
                    if th == 1:
                        pe.wait_ge(proj_copied, k + 1)
                    nc.tensor.matmul(ps[4 + k][:, :], wT[:, k // 2, P * (k % 2):P * (k % 2) + P], xnT[:, 512 * th:512 * th + 512],
                                     start=True, stop=True).then_inc(proj_ready, 1)
                for m in range(2 * th, 2 * th + 2):
                    if m >= 2:
                        pe.wait_ge(v_copied, m - 1)
                    for n in range(2):
                        t = 2 * m + n
                        last = nc.tensor.matmul(half_bank(m % 2)[:, 256 * n:256 * n + 256], xnT[:, P * t:P * t + P], wT[:, 2, :], start=True, stop=True)
                    last.then_inc(v_ready, 1)

            project_tokens(0)
            turn_tokens(1)
            project_tokens(1)

            def scores(n):
                if n == 0:
                    pe.wait_ge(proj_copied, 8)
                    pe.wait_ge(zeros_set, KVH)
                if n >= 4:
                    pe.wait_ge(s_biased, n - 3)
                for h in range(KVH):
                    last = nc.tensor.matmul(ps[4 + n % 4][:, P * h:P * h + P], qT[:, h, P * n:P * n + P],
                                            kT[:, h // 2, P * n:P * n + P], start=True, stop=True)
                last.then_inc(s_ready, 1)

            def turn_probs(n):
                pe.wait_ge(p_ready, n + 1)
                if n >= 2:
                    pe.wait_ge(pT_copied, n - 1)
                elif n == 0:
                    pe.wait_ge(v_copied, NTT // 2)
                for h in range(KVH):
                    last = nc.tensor.transpose(half_bank(n % 2)[:, P * h:P * h + P], pn[:, n % 2, h, :], ident)
                last.then_inc(pT_ready, 1)

            def attend(n):
                pe.wait_ge(pT_copied, n + 1)
                if n >= 2:
                    pe.wait_ge(keep.x2_ready, n - 1)
                for h in range(KVH):
                    r = DH * (h % 2)
                    last = nc.tensor.matmul(half_bank(2 + n % 2)[r:r + DH, P * (h // 2):P * (h // 2) + P], va[:, n, DH * h:DH * h + DH],
                                            prT[:, n % 2, P * h:P * h + P], start=True, stop=True, skip_group_check=True)
                last.then_inc(ao_ready, 1)

            def project_out(n):
                pe.wait_ge(ao_copied, n + 1)
                for h in range(2):
                    last = nc.tensor.matmul(half_bank(2 + n % 2)[:, 256:256 + P], aoT[:, n % 2, P * h:P * h + P], wT[:, 3, P * h:P * h + P],
                                            start=(h == 0), stop=(h == 1), skip_group_check=True)
                last.then_inc(y2_ready, 1)

            for n in range(NTT + 4):
                if n < NTT:
                    scores(n)
                if 2 <= n < NTT + 2:
                    turn_probs(n - 2)
                if 3 <= n < NTT + 3:
                    attend(n - 3)
                if n >= 4:
                    project_out(n - 4)

        @block.vector
        def _(dve):
            seq = [0]

            def link(op):
                seq[0] += 1
                op.then_inc(dve_seq, 1)
                dve.wait_ge(dve_seq, seq[0])

            dve.wait_ge(weights.landed, 16 * weights.count)
            link(nc.vector.tensor_reduce(rbm[:, :], weights.rel_bias.rearrange("b (g h) -> b h g", g=GA), axis=AX.X, op=ALU.add))
            nc.vector.tensor_scalar(rbm[:, :], rbm[:, :], 0.25, None, ALU.mult).then_inc(rbm_ready, 1)
            nc.vector.memset(bias[:, :, :], FAR).then_inc(far_set, 1)
            dve.wait_ge(rel_ready, 1)
            nc.vector.tensor_copy(rel[:, 0:2 * SQ - 1], ps[7][0:KVH, 0:2 * SQ - 1]).then_inc(rel_copied, 1)

            def normalise(m):
                dve.wait_ge(o_turned, m + 1)
                bank = wide[m % 2][:, :].rearrange("p (n a s c e) -> p n a s c e", n=2, a=2, s=2, c=4)
                for n in range(2):
                    for s in range(2):
                        op = nc.vector.reciprocal(rd[:, m % 2, n, s, :, :], bank[:, n, :, s, :, 16 * s + DK])
                link(op)
                for n in range(2):
                    for s in range(2):
                        op = nc.vector.tensor_tensor(on[:, 2 * m + n, :].rearrange("p (a c s d) -> p a c s d", a=2, c=4, s=2)[:, :, :, s, :],
                                                     bank[:, n, :, s, :, 16 * s:16 * s + DK],
                                                     rd[:, m % 2, n, s, :, :].unsqueeze(3).to_broadcast([P, 2, 4, DK]), ALU.mult)
                link(op)
                nc.vector.tensor_tensor(on[:, 2 * m:2 * m + 2, :], on[:, 2 * m:2 * m + 2, :], weights.bv.unsqueeze(1).to_broadcast([P, 2, P]),
                                        ALU.add).then_inc(o_normed, 1)

            def residual(m):
                dve.wait_ge(y1_ready, m + 1)
                if m == 0:
                    dve.wait_ge(bo_added, 1)
                nc.vector.tensor_tensor(x[:, 2 * m:2 * m + 2, :], x[:, 2 * m:2 * m + 2, :],
                                        ps[6 + m % 2][:, 0:2 * P].rearrange("p (n d) -> p n d", n=2), ALU.add).then_inc(x1_ready, 1)

            def statistics(hf):
                dve.wait_ge(x1_ready, 2 * hf + 2)
                for n in range(4 * hf, 4 * hf + 4):
                    last = nc.vector.bn_stats(bst[:, n, :], x[:, n, :])
                link(last)
                for n in range(4 * hf, 4 * hf + 4):
                    last = nc.vector.bn_aggr(bag[:, n, :], bst[:, n, :])
                last.then_inc(var_ready, 1)

            def norm(hf):
                dve.wait_ge(std_ready, hf + 1)
                h = 4 * hf
                link(nc.vector.reciprocal(rstd[:, h:h + 4], rstd[:, h:h + 4]))
                for n in range(h, h + 4):
                    nc.vector.tensor_scalar(xn[:, n, :], x[:, n, :], bag[:, n, 0:1], rstd[:, n:n + 1], ALU.subtract, ALU.mult).then_inc(xn_ready, 1)

            normalise(0)
            normalise(1)
            residual(0)
            normalise(2)
            residual(1)
            statistics(0)
            normalise(3)
            norm(0)
            residual(2)
            residual(3)
            statistics(1)
            dve.wait_ge(xnT_ready, 1)
            nc.vector.tensor_copy(xnT[:, 0:512], half_bank(2)).then_inc(xnT_copied, 1)
            norm(1)
            dve.wait_ge(bias_ready, 1)
            dve.wait_ge(far_set, 1)
            for a in range(2):
                op = nc.vector.tensor_copy(bias[64 * a:64 * a + 64, :, 64 * a:64 * a + 64],
                                           ps[5][64 * a:64 * a + 64, 0:256].rearrange("q (h k) -> q h k", h=KVH))
            op.then_inc(far_set, 1)
            dve.wait_ge(far_set, 2)

            def copy_values(m):
                dve.wait_ge(v_ready, m + 1)
                nc.vector.tensor_copy(va[:, 2 * m:2 * m + 2, :].rearrange("p n c -> p (n c)"), half_bank(m % 2)).then_inc(v_copied, 1)

            copy_values(0)
            copy_values(1)
            dve.wait_ge(xnT_ready, 2)
            nc.vector.tensor_copy(xnT[:, 512:1024], half_bank(3)).then_inc(xnT_copied, 1)
            copy_values(2)
            copy_values(3)

            for n in range(NTT + 4):
                if n < NTT:
                    dve.wait_ge(s_ready, n + 1)
                    nc.vector.tensor_tensor(sc[:, n, :, :], ps[4 + n % 4][:, :].rearrange("p (h k) -> p h k", h=KVH),
                                            bias[:, :, :], ALU.add).then_inc(s_biased, 1)
                    dve.wait_ge(s_biased, n + 1)
                    nc.vector.tensor_reduce(ngm[:, n, :], sc[:, n, :, :], axis=AX.X, op=ALU.max, negate=True).then_inc(max_ready, 1)
                if 1 <= n <= NTT:
                    dve.wait_ge(e_ready, n)
                    nc.vector.reciprocal(rden[:, n - 1, :], den[:, n - 1, :]).then_inc(rden_ready, 1)
                if 3 <= n < NTT + 3:
                    dve.wait_ge(ao_ready, n - 2)
                    nc.vector.tensor_copy(aoT[:, (n - 3) % 2, :], half_bank(2 + (n - 3) % 2)[:, 0:2 * P]).then_inc(ao_copied, 1)
                if n >= 4:
                    t = n - 4
                    dve.wait_ge(y2_ready, t + 1)
                    nc.vector.tensor_tensor(x[:, t, :], x[:, t, :], half_bank(2 + t % 2)[:, 256:256 + P], ALU.add).then_inc(keep.x2_ready, 1)
                    if t == NTT // 2:
                        dve.wait_ge(keep.x2_ready, NTT // 2)
                        for k in range(NTT // 2):
                            last = nc.vector.bn_stats(keep.stats[:, k, :], x[:, k, :])
                        link(last)
                        for k in range(NTT // 2):
                            last = nc.vector.bn_aggr(keep.mean_var[:, k, :], keep.stats[:, k, :])
                        last.then_inc(keep.var_ready, 1)


def experts(nc, io, keep):
    x, cst = keep.x, keep.constants
    ident = cst[:, 0:P]
    eps = cst[:, P + NG:P + NG + 1]
    with ExitStack() as ctx:
        def sb(name, shape, dt=F32):
            return ctx.enter_context(nc.sbuf_tensor(name, shape, dt))

        def sem(name):
            return ctx.enter_context(nc.semaphore(name))

        ew = keep.expert_weights
        w1, w2, b1r, b2, rw, rbb = ew.w1, ew.w2, ew.b1_rows, ew.b2, ew.router_w, ew.router_b
        c_landed, w1_landed, w2_landed = ew.small_landed, ew.w1_landed, ew.w2_landed
        bst, bag, rstd = keep.stats, keep.mean_var, keep.rstd
        w1h = sb("w1_hi", [P, 2, NHID], F32R)
        w1l = sb("w1_lo", [P, 2, NHID], F32R)
        xh = sb("x_normed_T_hi", [P, TOK], F32R)
        xl = sb("x_normed_T_lo", [P, TOK], F32R)
        b1 = sb("b1_cols", [P, NE * HC])
        xn = sb("x_normed_c", [P, NTT, D])
        xnT = sb("x_normed_T_c", [P, TOK])
        iota = sb("expert_numbers", [P, NE])
        lg = sb("logits", [P, NTT, NE])
        top = sb("top_values", [P, NTT, NE])
        idx = sb("top_indices", [P, NTT, NE], U32)
        idf = sb("top_indices_f", [P, NTT, NE])
        kp = sb("kept", [P, NTT, NE])
        eq = sb("second_kept", [P, NTT, NE])
        gs = sb("gate_sum", [P, NTT])
        gate = sb("gates", [P, NTT, NE])
        gT = sb("gates_T", [NE, TOK])
        hT = sb("hidden", [P, 2, HC, TOK])
        ps = [ctx.enter_context(nc.psum_tensor(f"moe_bank{i}", [P, 512], F32)) for i in range(8)]

        dve_seq = sem("moe_dve_seq")
        iota_ready = sem("iota_ready")
        b1_ready = sem("b1_ready")
        b1_copied = sem("b1_copied")
        act_passed = sem("act_passed")
        w1_split = sem("w1_split")
        w1_rounded = sem("w1_rounded")
        pool_passed = sem("moe_pool_passed")
        xh_ready = sem("xh_ready")
        xl_ready = sem("xl_ready")
        xn_ready = sem("moe_xn_ready")
        xnT_ready = sem("moe_xnT_ready")
        xnT_copied = sem("moe_xnT_copied")
        logits_ready = sem("logits_ready")
        shifted = sem("logits_shifted")
        exp_ready = sem("gates_exp_ready")
        gates_ready = sem("gates_ready")
        gT_ready = sem("gT_ready")
        gT_copied = sem("gT_copied")
        b2_ready = sem("b2_ready")
        h_ready = sem("h_ready")
        h_copied = sem("h_copied")
        y_ready = sem("y_ready")
        y_added = sem("y_added")
        stored = sem("out_stored")
        block = ctx.enter_context(nc.Block())

        @block.sync
        def _(sp):
            with sp.Fori(1, NE // 2) as i:
                for par in range(2):
                    e = 2 * i + par
                    sp.wait_ge(w1_split, e - 1)
                    sp.dma_start(w1[:, par, :], io["w1"][bass.ds(e, 1)].squeeze(0)).then_inc(w1_landed[par], 16)
                    sp.wait_ge(y_ready, 2 * (e - 1))
                    sp.dma_start(w2[:, par, :, :], io["w2"][bass.ds(e, 1)].squeeze(0).rearrange("(c p) n -> p c n", p=P)).then_inc(w2_landed[par], 16)
            out_d = io["out"].rearrange("b s d -> (b s) d").rearrange("(t p) d -> p t d", p=P)
            for g in range(2):
                sp.wait_ge(y_added, 2 * NE + g)
                sp.dma_start(out_d[:, 4 * g:4 * g + 4, :], x[:, 4 * g:4 * g + 4, :]).then_inc(stored, 16)
            sp.wait_ge(stored, 32)

        @block.gpsimd
        def _(pool):
            pool.iota(iota[:, :], pattern=[[1, NE]], base=0, channel_multiplier=0,
                      allow_small_or_imprecise_dtypes=True).then_inc(iota_ready, 1)

            def split(e, par):
                pool.wait_ge(w1_landed[par], 8 * (e - par) + 16)
                if not (isinstance(e, int) and e < 2):
                    pool.wait_ge(h_ready, 8 * (e - 1))
                pool.sem_inc(pool_passed, 1)
                pool.tensor_copy(w1h[:, par, :], w1[:, par, :]).then_inc(w1_rounded, 1)
                pool.wait_ge(w1_rounded, e + 1)
                pool.tensor_tensor(w1l[:, par, :], w1[:, par, :], w1h[:, par, :].bitcast(F32), ALU.subtract).then_inc(w1_split, 1)

            split(0, 0)
            split(1, 1)
            with pool.Fori(1, NE // 2) as i:
                split(2 * i, 0)
                split(2 * i + 1, 1)

        @block.scalar
        def _(act):
            act.wait_ge(keep.var_ready, 2)
            h = NTT // 2
            nc.scalar.activation(rstd[:, h:], bag[:, h:, 1], ACT.Sqrt, bias=eps).then_inc(keep.std_ready, 1)
            for k in range(2):
                act.wait_ge(xnT_ready, k + 1)
                nc.scalar.activation(xh[:, 512 * k:512 * k + 512], ps[k][:, :], ACT.Copy).then_inc(xh_ready, 1)
            act.wait_ge(b1_ready, 1)
            nc.scalar.activation(b1[:, :], ps[4][:, 0:NE * HC], ACT.Copy).then_inc(b1_copied, 1)
            act.wait_ge(b1_copied, 1)

            def relu(e, par):
                for k in range(8):
                    c, th = divmod(k, 2)
                    col = b1[:, HC * e + c:HC * e + c + 1] if isinstance(e, int) else b1[:, bass.ds(HC * e + c, 1)]
                    if k == 0 and not (isinstance(e, int) and e < 2):
                        act.wait_ge(y_ready, 2 * (e - 1))
                    act.wait_ge(h_ready, 8 * e + k + 1)
                    act.sem_inc(act_passed, 1)
                    nc.scalar.activation(hT[:, par, c, 512 * th:512 * th + 512], ps[(k + 2) % 4][:, :], ACT.Relu, bias=col).then_inc(h_copied, 1)

            relu(0, 0)
            act.wait_ge(shifted, 1)
            nc.scalar.activation(gate[:, :, :], lg[:, :, :], ACT.Exp).then_inc(exp_ready, 1)
            relu(1, 1)
            with act.Fori(1, NE // 2) as i:
                relu(2 * i, 0)
                relu(2 * i + 1, 1)

        @block.tensor
        def _(pe):
            pe.wait_ge(c_landed, 64)
            nc.tensor.transpose(ps[4][:, 0:NE * HC], b1r[:, :], ident[0:NE * HC, 0:NE * HC]).then_inc(b1_ready, 1)
            for n in range(NTT):
                pe.wait_ge(xn_ready, n + 1)
                last = nc.tensor.transpose(ps[n // 4][:, P * (n % 4):P * (n % 4) + P], xn[:, n, :], ident)
                if n % 4 == 3:
                    last.then_inc(xnT_ready, 1)

            def hidden(e, par):
                pe.wait_ge(w1_split, e + 1)
                for k in range(8):
                    c, th = divmod(k, 2)
                    if isinstance(e, int) and 8 * e + k < 4:
                        if k < 2:
                            pe.wait_ge(xl_ready, k + 1)
                        if k == 2:
                            pe.wait_ge(xnT_copied, 2)
                    else:
                        pe.wait_ge(h_copied, 8 * e + k - 3)
                    hi, lo = w1h[:, par, P * c:P * c + P], w1l[:, par, P * c:P * c + P]
                    cols = slice(512 * th, 512 * th + 512)
                    nc.tensor.matmul(ps[(k + 2) % 4][:, :], hi, xh[:, cols], start=True, stop=False)
                    nc.tensor.matmul(ps[(k + 2) % 4][:, :], hi, xl[:, cols], start=False, stop=False)
                    nc.tensor.matmul(ps[(k + 2) % 4][:, :], lo, xh[:, cols], start=False, stop=True).then_inc(h_ready, 1)

            def combine(e, par):
                pe.wait_ge(w2_landed[par], 8 * (e - par) + 16)
                pe.wait_ge(h_copied, 8 * e + 8)
                for g in range(2):
                    if not (isinstance(e, int) and e == 0):
                        pe.wait_ge(y_added, 2 * e + g)
                    for n in range(4 * g, 4 * g + 4):
                        for c in range(HC):
                            last = nc.tensor.matmul(ps[6 + g][:, P * (n % 4):P * (n % 4) + P], hT[:, par, c, P * n:P * n + P],
                                                    w2[:, par, c, :], start=(c == 0), stop=(c == HC - 1))
                    last.then_inc(y_ready, 1)

            hidden(0, 0)
            for n in range(NTT):
                last = nc.tensor.matmul(ps[5][:, NE * n:NE * n + NE], xnT[:, P * n:P * n + P], rw[:, :], start=True, stop=True)
            last.then_inc(logits_ready, 1)
            hidden(1, 1)
            pe.wait_ge(gates_ready, 1)
            for n in range(NTT):
                last = nc.tensor.transpose(ps[4 + n // 4][0:NE, P * (n % 4):P * (n % 4) + P], gate[:, n, :], ident)
            last.then_inc(gT_ready, 1)
            combine(0, 0)
            pe.wait_ge(gT_copied, 1)
            for n in range(NTT):
                last = nc.tensor.matmul(ps[4 + n // 4][:, P * (n % 4):P * (n % 4) + P], gT[:, P * n:P * n + P], b2[:, :], start=True, stop=True)
            last.then_inc(b2_ready, 1)
            with pe.Fori(1, NE // 2) as i:
                hidden(2 * i, 0)
                combine(2 * i - 1, 1)
                hidden(2 * i + 1, 1)
                combine(2 * i, 0)
            combine(NE - 1, 1)

        @block.vector
        def _(dve):
            seq = [0]

            def link(op):
                seq[0] += 1
                op.then_inc(dve_seq, 1)
                dve.wait_ge(dve_seq, seq[0])

            def norm(hf):
                dve.wait_ge(keep.std_ready, hf + 1)
                h = 4 * hf
                link(nc.vector.reciprocal(rstd[:, h:h + 4], rstd[:, h:h + 4]))
                for n in range(h, h + 4):
                    nc.vector.tensor_scalar(xn[:, n, :], x[:, n, :], bag[:, n, 0:1], rstd[:, n:n + 1], ALU.subtract, ALU.mult).then_inc(xn_ready, 1)

            dve.wait_ge(keep.x2_ready, NTT)
            for n in range(NTT // 2, NTT):
                last = nc.vector.bn_stats(bst[:, n, :], x[:, n, :])
            link(last)
            for n in range(NTT // 2, NTT):
                last = nc.vector.bn_aggr(bag[:, n, :], bst[:, n, :])
            last.then_inc(keep.var_ready, 1)
            norm(0)
            norm(1)
            for k in range(2):
                cols = slice(512 * k, 512 * k + 512)
                dve.wait_ge(xh_ready, k + 1)
                nc.vector.tensor_tensor(xl[:, cols], ps[k][:, :], xh[:, cols].bitcast(F32), ALU.subtract).then_inc(xl_ready, 1)
            for k in range(2):
                nc.vector.tensor_copy(xnT[:, 512 * k:512 * k + 512], ps[k][:, :]).then_inc(xnT_copied, 1)
            dve.wait_ge(c_landed, 64)
            dve.wait_ge(logits_ready, 1)
            link(nc.vector.tensor_tensor(lg[:, :, :], ps[5][:, 0:NTT * NE].rearrange("p (n e) -> p n e", e=NE),
                                         rbb[:, :].unsqueeze(1).to_broadcast([P, NTT, NE]), ALU.add))
            for n in range(NTT):
                op = nc.vector.max(top[:, n, :], lg[:, n, :])
            link(op)
            for n in range(NTT):
                op = nc.vector.max_index(idx[:, n, :], top[:, n, :], lg[:, n, :])
            link(op)
            link(nc.vector.tensor_copy(idf[:, :, :], idx[:, :, :]))
            nc.vector.tensor_tensor(lg[:, :, :], lg[:, :, :], top[:, :, 0:1].to_broadcast([P, NTT, NE]), ALU.subtract).then_inc(shifted, 1)
            dve.wait_ge(iota_ready, 1)
            numbers = iota[:, :].unsqueeze(1).to_broadcast([P, NTT, NE])
            nc.vector.tensor_tensor(kp[:, :, :], numbers, idf[:, :, 0:1].to_broadcast([P, NTT, NE]), ALU.is_equal)
            link(nc.vector.tensor_tensor(eq[:, :, :], numbers, idf[:, :, 1:2].to_broadcast([P, NTT, NE]), ALU.is_equal))
            link(nc.vector.tensor_tensor(kp[:, :, :], kp[:, :, :], eq[:, :, :], ALU.add))
            dve.wait_ge(exp_ready, 1)
            link(nc.vector.tensor_tensor(gate[:, :, :], gate[:, :, :], kp[:, :, :], ALU.mult))
            link(nc.vector.tensor_reduce(gs[:, :], gate[:, :, :], axis=AX.X, op=ALU.add))
            link(nc.vector.reciprocal(gs[:, :], gs[:, :]))
            nc.vector.tensor_tensor(gate[:, :, :], gate[:, :, :], gs[:, :].unsqueeze(2).to_broadcast([P, NTT, NE]), ALU.mult).then_inc(gates_ready, 1)
            def add(e):
                for g in range(2):
                    dve.wait_ge(y_ready, 2 * e + g + 1)
                    if not isinstance(e, int):
                        dve.wait_ge(y_added, 2 * e + g)
                    for n in range(4 * g, 4 * g + 4):
                        col = gate[:, n, e:e + 1] if isinstance(e, int) else gate[:, n, bass.ds(e, 1)]
                        op = nc.vector.scalar_tensor_tensor(out=x[:, n, :], in0=ps[6 + g][:, P * (n % 4):P * (n % 4) + P], scalar=col,
                                                            in1=x[:, n, :], op0=ALU.mult, op1=ALU.add)
                    op.then_inc(y_added, 1)

            dve.wait_ge(gates_ready, 1)
            dve.wait_ge(gT_ready, 1)
            for k in range(2):
                op = nc.vector.tensor_copy(gT[:, 512 * k:512 * k + 512], ps[4 + k][0:NE, :])
            op.then_inc(gT_copied, 1)
            add(0)
            dve.wait_ge(b2_ready, 1)
            dve.wait_ge(y_added, 2)
            for k in range(2):
                op = nc.vector.tensor_tensor(x[:, 4 * k:4 * k + 4, :], x[:, 4 * k:4 * k + 4, :], ps[4 + k][:, :].rearrange("p (n d) -> p n d", n=4), ALU.add)
            op.then_inc(y_added, 1)
            dve.wait_ge(y_added, 3)
            with dve.Fori(0, NE - 1) as i:
                add(i + 1)


class Kept:
    pass


class AttentionWeights:

    def __init__(self, context, tail, mask_raw, landed):
        flat = context[:, :, :, :, :].rearrange("p a c j d -> p (a c j d)")
        self.qkv = flat.rearrange("p (w g m) -> p w g m", w=3, g=GA)
        raw = mask_raw[:, :].bitcast(F32)
        self.o = raw[:, 0:1024].rearrange("p (g c) -> p g c", g=GA)
        self.out1 = raw[:, 1024:1152]
        self.bv = raw[:, 1152:1280]
        self.bo = raw[:, 1280:1408]
        self.flip = raw[0:SQ, 1408:1536]
        self.rel_bias = raw[0:NBKT, 1536:1552]
        self.onehot = tail[0:NBKT, 0, 0:2 * SQ - 1]
        self.landed = landed
        self.count = 10

    def load(self, sp, io):
        for k, name in enumerate(("aWq", "aWk", "aWv")):
            sp.dma_start(self.qkv[:, k, :, :].rearrange("r g (h m) -> r (g h) m", h=2),
                         io[name].rearrange("(b r) m -> r b m", r=P)).then_inc(self.landed, 16)
        sp.dma_start(self.onehot, io["bucket_onehot"]).then_inc(self.landed, 16)

    def load_rest(self, sp, io):
        sp.dma_start(self.o.rearrange("p g c -> p (g c)"), io["aWo"]).then_inc(self.landed, 16)
        sp.dma_start(self.out1, io["Wo"]).then_inc(self.landed, 16)
        sp.dma_start(self.bv, io["bv"].unsqueeze(0).to_broadcast([P, P])).then_inc(self.landed, 16)
        sp.dma_start(self.bo, io["bo"].unsqueeze(0).to_broadcast([P, P])).then_inc(self.landed, 16)
        sp.dma_start(self.flip, io["flip"]).then_inc(self.landed, 16)
        sp.dma_start(self.rel_bias, io["rel_bias"]).then_inc(self.landed, 16)


class ExpertWeights:

    def __init__(self, sb, sem):
        self.w1 = sb("w1", [P, 2, NHID])
        self.w2 = sb("w2", [P, 2, HC, D])
        self.b1_rows = sb("b1_rows", [NE * HC, P])
        self.b2 = sb("b2", [NE, D])
        self.router_w = sb("router_w", [P, NE])
        self.router_b = sb("router_b_rows", [P, NE])
        self.small_landed = sem("moe_small_landed")
        self.w1_landed = [sem(f"w1_landed{i}") for i in range(2)]
        self.w2_landed = [sem(f"w2_landed{i}") for i in range(2)]

    def load_first(self, sp, io):
        sp.dma_start(self.router_w[:, :], io["router_w"]).then_inc(self.small_landed, 16)
        sp.dma_start(self.router_b[:, :], io["router_b"].unsqueeze(0).to_broadcast([P, NE])).then_inc(self.small_landed, 16)
        sp.dma_start(self.b1_rows[:, :], io["b1"].rearrange("e (c p) -> (e c) p", p=P)).then_inc(self.small_landed, 16)
        sp.dma_start(self.b2[:, :], io["b2"]).then_inc(self.small_landed, 16)
        for e in range(2):
            sp.dma_start(self.w1[:, e, :], io["w1"][e]).then_inc(self.w1_landed[e], 16)
            sp.dma_start(self.w2[:, e, :, :], io["w2"][e].rearrange("(c p) n -> p c n", p=P)).then_inc(self.w2_landed[e], 16)


def perceiver_program(nc, io):
    keep = Kept()
    with ExitStack() as ctx:
        def sb(name, shape, dt=F32):
            return ctx.enter_context(nc.sbuf_tensor(name, shape, dt))

        keep.ou = sb("outs", [P, NTT, 4, 2, SQ])
        keep.x = sb("x_tokens", [P, NTT, D])
        keep.constants = sb("constants", [P, P + NG + 1])
        keep.ones = sb("ones", [P, 1])
        keep.context = sb("context", [P, 2, 3, 4, D])
        keep.tail = sb("context_tail", [TAIL, 2, D])
        keep.mask_raw = sb("mask_raw", [P, SK], I32)
        keep.x2_ready = ctx.enter_context(nc.semaphore("x2_ready"))
        keep.weights = AttentionWeights(keep.context, keep.tail, keep.mask_raw, ctx.enter_context(nc.semaphore("attn_w_landed")))
        cross_attention(nc, io, keep)
        keep.expert_weights = ExpertWeights(sb, lambda name: ctx.enter_context(nc.semaphore(name)))
        keep.stats = sb("ln_stats_c", [P, NTT, 6])
        keep.mean_var = sb("ln_aggr_c", [P, NTT, 2])
        keep.rstd = sb("ln_rstd_c", [P, NTT])
        keep.var_ready = ctx.enter_context(nc.semaphore("moe_var_ready"))
        keep.std_ready = ctx.enter_context(nc.semaphore("moe_std_ready"))
        self_attention(nc, io, keep)
        experts(nc, io, keep)


def shape_constants():
    import numpy as np

    table = np.zeros((P, P + NG + 1), np.float32)
    table[:, 0:P] = np.eye(P)
    for p in range(KS):
        table[p, P + p % 32 // DK] = 1.0
    table[:, P + NG] = EPS
    rel = np.arange(2 * SQ - 1) - (SQ - 1)
    dist = np.abs(rel)
    half, exact = NBKT // 2, NBKT // 4
    far = exact + (np.log(np.maximum(dist, 1).astype(np.float32) / np.float32(exact)) / np.float32(np.log(128 / exact))
                   * np.float32(half - exact)).astype(np.int32)
    bucket = np.where(rel > 0, half, 0) + np.where(dist < exact, dist, np.minimum(far, half - 1))
    onehot = (np.arange(NBKT)[:, None] == bucket[None, :]).astype(np.float32)
    flip = np.zeros((SQ, P), np.float32)
    flip[SQ - 1 - np.arange(P) % SQ, np.arange(P)] = 1.0
    return {"constants": table, "bucket_onehot": onehot, "flip": flip}


_INS = {"x": "x", "ctx_1024": "ctx", "mask_BxSxS2_if1": "mask", "L0_xattn_Wq": "Wq", "L0_xattn_bq": "bq",
        "L0_xattn_Wk": "Wk", "L0_xattn_bk": "bk", "L0_xattn_Wv": "Wv", "L0_xattn_bv": "bv", "L0_xattn_Wo": "Wo",
        "L0_xattn_bo": "bo", "L0_attn_Wq": "aWq", "L0_attn_Wk": "aWk", "L0_attn_Wv": "aWv", "L0_attn_Wo": "aWo",
        "L0_attn_rel_bias": "rel_bias", "L0_ffn_router_w": "router_w", "L0_ffn_router_b": "router_b",
        "L0_ffn_w1": "w1", "L0_ffn_b1": "b1", "L0_ffn_w2": "w2", "L0_ffn_b2": "b2"}


def kernel(**inputs):
    import numpy as _np
    import concourse.bacc as _bacc
    from concourse.bass_utils import run_bass_kernel_spmd as _run

    nc = _bacc.Bacc("TRN2", target_bir_lowering=False, num_devices=1)
    arrays, io = {}, {}
    for name, short in _INS.items():
        arrays[f"in_{name}"] = a = _np.ascontiguousarray(inputs[name])
        io[short] = nc.dram_tensor(f"in_{name}", a.shape, mybir.dt.from_np(a.dtype), kind="ExternalInput").ap()
    for name, a in shape_constants().items():
        arrays[f"shape_{name}"] = a
        io[name] = nc.dram_tensor(f"shape_{name}", a.shape, mybir.dt.from_np(a.dtype), kind="ExternalInput").ap()
    io["out"] = nc.dram_tensor("out", (B, SQ, D), F32, kind="ExternalOutput").ap()
    perceiver_program(nc, io)
    r = _run(nc, [arrays], core_ids=[0])
    return r.results[0]["out"]
```
